# Optimizing a Trainium2 kernel written in Bass

```python
import numpy as np
import jax
import jax.numpy as jnp

def _softmax(x, axis=-1):
    return jax.nn.softmax(x, axis=axis)

def _gelu(x):
    return jax.nn.gelu(x, approximate=True)

def _silu(x):
    return jax.nn.silu(x)

def _sigmoid(x):
    return jax.nn.sigmoid(x)

def _layernorm(x, axis=-1, eps=1e-05):
    m = jnp.mean(x, axis=axis, keepdims=True)
    v = jnp.var(x, axis=axis, keepdims=True)
    return (x - m) / jnp.sqrt(v + eps)

def _scatter_add(tgt, idx, src, axis=0):
    return tgt.at[idx].add(src)

def _segment_sum(src, seg, n):
    return jax.ops.segment_sum(src, seg, n)
kernel_name = 'mk_gnn_ffn_d1_gnn_r8_bdf687'

def setup_inputs(seed: int=0):
    np.random.seed(seed)
    _w = jnp.asarray

    def _rec_inputs():
        import jax
        import jax.numpy as jnp
        _gk = jax.random.key(seed)
        x = -0.0002117 + 1 * jax.random.normal(jax.random.fold_in(_gk, 1), (1250, 512), jnp.float32)
        _s = jax.random.randint(jax.random.fold_in(_gk, 2), (20000,), 0, 1250, jnp.int32)
        _d = jax.random.randint(jax.random.fold_in(_gk, 3), (20000,), 0, 1250, jnp.int32)
        _loop = jnp.arange(1250, dtype=jnp.int32)
        src = jnp.concatenate([_s, _d, _loop])
        dst = jnp.concatenate([_d, _s, _loop])
        _o = jnp.argsort(dst, stable=True)
        src = src[_o]
        dst = dst[_o]
        edge_weight = jax.random.uniform(jax.random.fold_in(_gk, 12), (41250,), jnp.float32, 0.0, 0.999996)
        return (x, src, dst, edge_weight)
    x, src, dst, edge_weight = _rec_inputs()

    def _L0_gnn_setup():
        import jax, jax.numpy as jnp
        import numpy as np
        N_NODES = 6250
        N_EDGES = 20000
        DIM = 512

        def gcn_conv(x, src, dst, edge_weight, W, b, num_nodes):
            loop = jnp.arange(num_nodes, dtype=src.dtype)
            s = jnp.concatenate([src, loop])
            d = jnp.concatenate([dst, loop])
            w = jnp.concatenate([edge_weight, jnp.ones((num_nodes,), x.dtype)])
            deg = jax.ops.segment_sum(w, d, num_segments=num_nodes)
            dis = jnp.where(deg > 0, jax.lax.rsqrt(jnp.where(deg > 0, deg, 1.0)), 0.0)
            norm = dis[s] * w * dis[d]
            h = x @ W
            msg = h[s] * norm[:, None]
            out = jax.ops.segment_sum(msg, d, num_segments=num_nodes)
            return out + b
        key = jax.random.key(seed)
        ks = jax.random.split(key, 6)
        x = jax.random.normal(ks[0], (N_NODES, DIM), jnp.float32)
        edge_index = jax.random.randint(ks[1], (2, N_EDGES), 0, N_NODES, dtype=jnp.int64)
        edge_attr = jax.random.uniform(ks[2], (N_EDGES,), jnp.float32)
        W1 = jax.random.normal(ks[3], (DIM, DIM), jnp.float32) * (1.0 / np.sqrt(DIM))
        b1 = jnp.zeros((DIM,), jnp.float32)
        W2 = jax.random.normal(ks[4], (DIM, DIM), jnp.float32) * (1.0 / np.sqrt(DIM))
        b2 = jnp.zeros((DIM,), jnp.float32)
        return {'x': x, 'edge_index': edge_index, 'edge_attr': edge_attr, 'W1': W1, 'b1': b1, 'W2': W2, 'b2': b2}
    _L0_gnn_all = _L0_gnn_setup()
    _L0_gnn_in = {k: v for k, v in _L0_gnn_all.items() if k in ('W1', 'b1', 'W2', 'b2')}
    del _L0_gnn_all

    def _L0_ffn_setup():
        import jax, jax.numpy as jnp
        import numpy as np
        B, T, C = (8, 1024, 512)
        H = 1024
        G, EG = (2, 4)
        E = G * EG
        K = 2
        LN_EPS = 1e-05

        def _swiglu(x):
            a, b = jnp.split(x, 2, axis=-1)
            return jax.nn.silu(a) * b
        key = jax.random.key(seed)
        ks = jax.random.split(key, 8)
        n = lambda k, shape, s: jax.random.normal(k, shape, dtype=jnp.float32) * s
        return {'x': n(ks[0], (B, T, C), 1.0), 'ln_scale': jnp.ones((C,), jnp.float32), 'ln_bias': jnp.zeros((C,), jnp.float32), 'shared_in_w': n(ks[1], (2 * H, C), 0.02), 'shared_out_w': n(ks[2], (C, H), 0.02), 'shared_out_b': jnp.zeros((C,), jnp.float32), 'expert_in_w': n(ks[3], (2 * H, C), 0.02), 'expert_out_weight': n(ks[4], (E, C, H), 0.02), 'expert_out_bias': jnp.zeros((E, C), jnp.float32), 'group_gate_w': n(ks[5], (G, C), 0.02), 'expert_gate_w': n(ks[6], (E, C), 0.02), 'group_bias': jnp.zeros((G,), jnp.float32), 'expert_bias': jnp.zeros((E,), jnp.float32)}
    _L0_ffn_all = _L0_ffn_setup()
    _L0_ffn_in = {k: v for k, v in _L0_ffn_all.items() if k in ('ln_scale', 'ln_bias', 'shared_in_w', 'shared_out_w', 'shared_out_b', 'expert_in_w', 'expert_out_weight', 'expert_out_bias', 'group_gate_w', 'expert_gate_w', 'group_bias', 'expert_bias')}
    del _L0_ffn_all
    return {'x': x, 'src': src, 'dst': dst, 'edge_weight': edge_weight, 'L0_gnn_W1': _L0_gnn_in['W1'], 'L0_gnn_b1': _L0_gnn_in['b1'], 'L0_gnn_W2': _L0_gnn_in['W2'], 'L0_gnn_b2': _L0_gnn_in['b2'], 'L0_ffn_ln_scale': _L0_ffn_in['ln_scale'], 'L0_ffn_ln_bias': _L0_ffn_in['ln_bias'], 'L0_ffn_shared_in_w': _L0_ffn_in['shared_in_w'], 'L0_ffn_shared_out_w': _L0_ffn_in['shared_out_w'], 'L0_ffn_shared_out_b': _L0_ffn_in['shared_out_b'], 'L0_ffn_expert_in_w': _L0_ffn_in['expert_in_w'], 'L0_ffn_expert_out_weight': _L0_ffn_in['expert_out_weight'], 'L0_ffn_expert_out_bias': _L0_ffn_in['expert_out_bias'], 'L0_ffn_group_gate_w': _L0_ffn_in['group_gate_w'], 'L0_ffn_expert_gate_w': _L0_ffn_in['expert_gate_w'], 'L0_ffn_group_bias': _L0_ffn_in['group_bias'], 'L0_ffn_expert_bias': _L0_ffn_in['expert_bias']}

def reference(x, src, dst, edge_weight, L0_gnn_W1, L0_gnn_b1, L0_gnn_W2, L0_gnn_b2, L0_ffn_ln_scale, L0_ffn_ln_bias, L0_ffn_shared_in_w, L0_ffn_shared_out_w, L0_ffn_shared_out_b, L0_ffn_expert_in_w, L0_ffn_expert_out_weight, L0_ffn_expert_out_bias, L0_ffn_group_gate_w, L0_ffn_expert_gate_w, L0_ffn_group_bias, L0_ffn_expert_bias):
    import jax
    import jax.numpy as jnp

    def _L0_gnn_ref(x, edge_index, edge_attr, W1, b1, W2, b2):
        import jax, jax.numpy as jnp
        import numpy as np
        N_NODES = 6250
        N_EDGES = 20000
        DIM = 512

        def gcn_conv(x, src, dst, edge_weight, W, b, num_nodes):
            loop = jnp.arange(num_nodes, dtype=src.dtype)
            s = jnp.concatenate([src, loop])
            d = jnp.concatenate([dst, loop])
            w = jnp.concatenate([edge_weight, jnp.ones((num_nodes,), x.dtype)])
            deg = jax.ops.segment_sum(w, d, num_segments=num_nodes)
            dis = jnp.where(deg > 0, jax.lax.rsqrt(jnp.where(deg > 0, deg, 1.0)), 0.0)
            norm = dis[s] * w * dis[d]
            h = x @ W
            msg = h[s] * norm[:, None]
            out = jax.ops.segment_sum(msg, d, num_segments=num_nodes)
            return out + b
        src, dst = (edge_index[0], edge_index[1])
        n = x.shape[0]
        h = gcn_conv(x, src, dst, edge_attr, W1, b1, n)
        h = jax.nn.relu(h)
        ones = jnp.ones((src.shape[0],), x.dtype)
        out = gcn_conv(h, src, dst, ones, W2, b2, n)
        return out

    def _L0_ffn_ref(x, ln_scale, ln_bias, shared_in_w, shared_out_w, shared_out_b, expert_in_w, expert_out_weight, expert_out_bias, group_gate_w, expert_gate_w, group_bias, expert_bias):
        import jax, jax.numpy as jnp
        import numpy as np
        B, T, C = (8, 1024, 512)
        H = 1024
        G, EG = (2, 4)
        E = G * EG
        K = 2
        LN_EPS = 1e-05

        def _swiglu(x):
            a, b = jnp.split(x, 2, axis=-1)
            return jax.nn.silu(a) * b
        Bx, Tx, Cx = x.shape
        S = Bx * Tx
        flat = x.reshape(S, Cx)
        mu = flat.mean(-1, keepdims=True)
        var = ((flat - mu) ** 2).mean(-1, keepdims=True)
        flat = (flat - mu) * jax.lax.rsqrt(var + LN_EPS) * ln_scale + ln_bias
        h_shared = _swiglu(flat @ shared_in_w.T)
        out_shared = h_shared @ shared_out_w.T + shared_out_b
        g_logits = flat @ group_gate_w.T + group_bias
        g_idx = jnp.argmax(g_logits, axis=-1)
        e_logits = (flat @ expert_gate_w.T).reshape(S, G, EG)
        e_sel = jnp.take_along_axis(e_logits, g_idx[:, None, None], axis=1)[:, 0, :]
        e_sel = e_sel + expert_bias.reshape(G, EG)[g_idx]
        e_probs = jax.nn.softmax(e_sel, axis=-1)
        topv, topi = jax.lax.top_k(e_probs, K)
        topv = topv / (topv.sum(-1, keepdims=True) + 1e-08)
        disp = g_idx[:, None] * EG + topi
        h_expert = _swiglu(flat @ expert_in_w.T)
        rows = jnp.arange(S)[:, None]
        comb = jnp.zeros((S, E), flat.dtype).at[rows, disp].add(topv)
        cnt = jnp.zeros((S, E), flat.dtype).at[rows, disp].add(1.0)
        routed = cnt @ expert_out_bias
        for e in range(E):
            routed = routed + comb[:, e:e + 1] * (h_expert @ expert_out_weight[e].T)
        return (out_shared + routed).reshape(Bx, Tx, Cx)
    edge_index = jnp.stack([src, dst])
    x = x + _L0_gnn_ref(_layernorm(x, axis=-1), edge_index, edge_weight, L0_gnn_W1, L0_gnn_b1, L0_gnn_W2, L0_gnn_b2)
    x = x + _L0_ffn_ref(_layernorm(x, axis=-1)[None], L0_ffn_ln_scale, L0_ffn_ln_bias, L0_ffn_shared_in_w, L0_ffn_shared_out_w, L0_ffn_shared_out_b, L0_ffn_expert_in_w, L0_ffn_expert_out_weight, L0_ffn_expert_out_bias, L0_ffn_group_gate_w, L0_ffn_expert_gate_w, L0_ffn_group_bias, L0_ffn_expert_bias)[0]
    return x

_drawn_inputs = setup_inputs


def setup_inputs(seed=0):
    import zlib

    import numpy as np

    out = dict(_drawn_inputs(seed))
    spreads = {'L0_gnn_b1': (0.0, 0.1),
     'L0_gnn_b2': (0.0, 0.1),
     'L0_ffn_ln_scale': (1.0, 0.2),
     'L0_ffn_ln_bias': (0.0, 0.1),
     'L0_ffn_shared_out_b': (0.0, 0.1),
     'L0_ffn_expert_out_bias': (0.0, 0.1),
     'L0_ffn_group_bias': (0.0, 0.1),
     'L0_ffn_expert_bias': (0.0, 0.1)}
    factors = {}
    for name, (base, spread) in spreads.items():
        noise = np.random.default_rng([zlib.crc32(name.encode()), seed]).standard_normal(out[name].shape)
        drawn = base * np.exp(spread * noise) if base else spread * noise
        out[name] = jnp.asarray(drawn.astype(out[name].dtype))
    for name, factor in factors.items():
        out[name] = (out[name] * factor).astype(out[name].dtype)
    return out
```

```python
import concourse.bass as bass
from concourse import mybir
from contextlib import ExitStack

NODES, DIM, EDGES = 1250, 512, 41250
PT = 125
NT = NODES // PT
CT = DIM // 128
CH = 128
NCH = 324
CG = NCH // 3
DW = 16
NWIN = -(-NODES // DW)
DPAD = NWIN * DW
SLO = NODES // 2
HW2 = 313
SLP = 2 * HW2
KEYS = 2 * DW
NQ = 4
AHEAD = 2
NB = 4
HID = 1024
NE = 8
WS = 64.0
HS = 16.0
LNEPS = 1e-5


def gnn_ffn_kernel(nc, io, out, debug=None):
    f32, i32, i16 = mybir.dt.float32, mybir.dt.int32, mybir.dt.int16
    bf16, f16 = mybir.dt.bfloat16, mybir.dt.float16
    ALU = mybir.AluOpType
    ACT = mybir.ActivationFunctionType
    AX = mybir.AxisListType
    ds = bass.ds

    ctx = ExitStack()
    with ctx:
        size_of = {f32: 4, i32: 4, i16: 2, bf16: 2, f16: 2}
        base = 16512

        class Region:
            def __init__(self, start, size):
                self.at, self.end, self.start = start, start + size, start

            def __call__(self, name, shape, dt):
                n = size_of[dt]
                for s in shape[1:]:
                    n *= s
                t = nc.alloc_sbuf_tensor_at(name, shape, dt, offset=self.at)
                self.at += -(-n // 32) * 32
                assert self.at <= self.end, (name, self.at - self.start, self.end - self.start)
                return t

        def region(size):
            nonlocal base
            r = Region(base, size)
            base += size
            return r

        keep = region(20480 + 8704+256)
        slots = region(NE * 16384)
        share = region(40960)
        stage = region(212832 - base + 16512)

        def pb(name, banks=1, dt=f32):
            n = 512 * banks if dt == f32 else 1024 * banks
            return ctx.enter_context(nc.psum_tensor(name, [128, n], dt))

        def sem(name):
            return ctx.enter_context(nc.semaphore(name))

        x_sb = keep("x_sb", [PT, NT, DIM], f32)
        identf = keep("identf", [128, 128], f32)
        ident = keep("ident", [128, 128], f16)
        onesf = keep("onesf", [CG, NWIN], f32)

        AT_h = nc.alloc_sbuf_tensor_at("AT_h", [PT, NT, 2, DPAD], f16, offset=slots.start)
        AT_l = nc.alloc_sbuf_tensor_at("AT_l", [PT, NT, 2, DPAD], f16, offset=slots.start + NT * 2 * DPAD * 2)
        slots.at += NT * 2 * DPAD * 2 * 2
        e_src = share("e_src", [CH, NCH], i32)
        e_dst = share("e_dst", [CH, NCH], i32)
        e_w = share("e_w", [CH, NCH], f32)
        dst_c = share("dst_c", [CG, 3, CH], i32)
        slo_f = share("slo_f", [CH, NCH], f32)
        key_f = share("key_f", [CH, NCH], f32)
        wq = share("wq", [CH, NCH, NQ], bf16)
        scr0 = share("scr0", [CH, NCH], f32)
        scr1 = share("scr1", [CH, NCH], f32)
        oh_src = share("oh_src", [CH, NB * SLP], bf16)
        oh_key = share("oh_key", [CH, NB * 128], bf16)
        iota_s = share("iota_s", [CH, SLP], i16)
        iota_k = share("iota_k", [CH, NWIN * KEYS], i16)
        R = [share(f"R{i}", [128, SLP], f32) for i in range(2)]
        T = [slots(f"T{i}", [PT, 5 * 2 * KEYS], f32) for i in range(2)]
        comb = slots("comb", [128, 2 * KEYS], f32)
        tri = slots("tri", [128, 128], f32)
        dmm = slots("dmm", [CG, 6], f32)
        diag = slots("diag", [CG, 6, CG], f32)
        c_up = share("c_up", [NWIN, NCH], f32)
        c_dn = share("c_dn", [NWIN, NCH], f32)
        hit = slots("hit", [NWIN, NCH], f32)
        hit2 = slots("hit2", [NWIN, NCH], f32)
        wlim = slots("wlim", [NWIN, 2], f32)
        rcol = slots("rcol", [NWIN, 4], f32)
        pmark = keep("pmark", [1, 1], f32)
        amark = keep("amark", [1, 2], f32)
        scr_mark = keep("scr_mark", [1, 4], f32)
        rng = keep("rng", [1, NWIN * 4], i32)

        g_share = Region(share.start, 40960)
        xs = g_share("xs", [PT, NT, 2, DIM], f16)
        aggT = g_share("aggT", [128, CT, 2, NODES], f16)
        W = [slots(f"W{i}", [128, CT, 2, DIM], f16) for i in range(2)]
        xt = [slots(f"xt{i}", [PT, DIM], f32) for i in range(2)]
        raw = [stage(f"raw{i}", [128, 1024], f32) for i in range(2)]
        f_share = Region(share.start, 40960)
        zf = f_share("zf", [PT, NT, DIM], f32)
        vt = [f_share(f"vt{i}", [128, CT * PT], f32) for i in range(2)]
        h_share = Region(share.start, 40960)
        hT = [h_share("hT_shared", [128, 8, 2, NODES], f16)]
        f_slots = Region(slots.start, NE * 16384)
        hT.append(f_slots("hT_expert", [128, 8, 2, NODES], f16))
        flatT = f_slots("flatT", [128, CT, 2, NODES], f16)
        o_slots = Region(f_slots.at, 65536)
        inW = [f_slots(f"inW{i}", [128, CT, 2, 2 * HID], f16) for i in (1, 0)][::-1]
        outW = [o_slots(f"outW{i}", [128, 8, 2, DIM], f16) for i in range(3)]
        sl = [f_slots(f"sl{i}", [128, 500], f32) for i in range(2)]
        b_bc = [keep(f"b_bc{i}", [PT, DIM], f32) for i in range(2)]
        lnw = keep("lnw", [128, 2, CT], f32)
        gate_raw = stage("gate_raw", [128, CT, 10], f32)
        gate = stage("gate", [128, CT, 2, 10], f16)
        gb10 = stage("gb10", [PT, 10], f32)
        st6 = stage("st6", [PT, NT, 6], f32)
        mv = stage("mv", [PT, NT, 2], f32)
        rs = stage("rs", [PT, NT], f32)
        rv = stage("rv", [PT, 2 * NT], f32)
        rw = stage("rw", [PT, 2 * NT], f32)
        rx = stage("rx", [PT, 2 * NT], f32)
        pos = stage("pos", [PT, 2 * NT], f32)
        dis = stage("dis", [PT, 2 * NT], f32)
        dsc = stage("dsc", [PT, 2 * NT], f32)
        ones16 = stage("ones16", [PT, 1], f16)
        cnt9 = keep("cnt9", [PT, NT, 9], f32)
        c_slots = Region(f_slots.start + 40000, 20000)
        cntT = c_slots("cntT", [9, NODES], f32)
        bias9 = c_slots("bias9", [9, DIM], f32)
        comb8 = keep("comb8", [PT, NT, NE], f32)
        lg = keep("lg", [PT, NT, 10], f32)
        e4 = [keep(f"e4_{i}", [PT, NT, 4], f32) for i in range(4)]
        r1 = [keep(f"r1_{i}", [PT, NT], f32) for i in range(5)]
        i4 = keep("i4", [PT, 4], f32)

        psR = [pb(f"psR{i}", 2) for i in range(2)]
        psT = [pb(f"psT{i}") for i in range(2)]
        psX = [pb(f"psX{i}") for i in range(2)]

        s_edge = [sem(f"s_edge{i}") for i in range(4)]
        s_const = sem("s_const")
        s_pc = sem("s_pc")
        s_vc = sem("s_vc")
        s_dmm = sem("s_dmm")
        s_bc = sem("s_bc")
        s_rcol = sem("s_rcol")
        s_rrow = sem("s_rrow")
        s_rng = sem("s_rng")
        oh_ready = sem("oh_ready")
        oh_free = sem("oh_free")
        r_full = sem("r_full")
        r_copied = sem("r_copied")
        t_full = sem("t_full")
        t_copied = sem("t_copied")
        at_hi = sem("at_hi")
        at_ready = sem("at_ready")
        s_dbg = sem("s_dbg")
        s_x = sem("s_x")
        s_bias = sem("s_bias")
        s_small = sem("s_small")
        s_w = [sem(f"s_w{i}") for i in range(2)]
        w_hi = sem("w_hi")
        w_lo = sem("w_lo_done")
        s_sqin = sem("s_sqin")
        s_sqout = sem("s_sqout")
        s_deg = sem("s_deg")
        xt_ready = sem("xt_ready")
        xs_hi = sem("xs_hi")
        xs_lo = sem("xs_lo")
        agg_full = sem("agg_full")
        agg_hi = sem("agg_hi")
        agg_lo = sem("agg_lo")
        lin_full = sem("lin_full")
        lin_read = sem("lin_read")
        zf_ready = sem("zf_ready")
        tr_full = sem("tr_full")
        vt_ready = sem("vt_ready")
        fl_hi = sem("fl_hi")
        fl_lo = sem("fl_lo")
        s_logit = sem("s_logit")
        s_lg = sem("s_lg")
        s_exin = sem("s_exin")
        s_exout = sem("s_exout")
        s_route = sem("s_route")
        in_full = sem("in_full")
        in_silu = sem("in_silu")
        in_h = sem("in_h")
        h_hi = sem("h_hi")
        h_lo = sem("h_lo")
        s_cntT = sem("s_cntT")
        s_cntTc = sem("s_cntTc")
        out_full = sem("out_full")
        out_read = sem("out_read")
        s_final = sem("s_final")
        s_out = sem("s_out")

        agg_ps = [(psR[i], psT[i]) for i in range(2)]
        in_ps = [psR[i] for i in range(2)]
        SPANS = [(0, 500), (500, 500), (1000, 250)]
        P_W, P_IN, P_OUT, P_EXP = 0, 4, 20, 24

        block = ctx.enter_context(nc.Block())

        @block.sync
        def _(sp):
            sp.dma_start(e_dst[:, :], io["e_dst"]).then_inc(s_edge[0], 16)
            sp.dma_start(dst_c[:, :, :], io["dst_c"]).then_inc(s_edge[1], 16)
            sp.dma_start(e_src[:, :], io["e_src"]).then_inc(s_edge[2], 16)
            sp.dma_start(e_w[:, :], io["e_w"]).then_inc(s_edge[3], 16)
            sp.dma_start(x_sb[:, :, :], io["x"]).then_inc(s_x, 16)
            for dst_t, name in ((b_bc[0], "b1"), (b_bc[1], "b2"), (gb10, "gb10")):
                sp.dma_start(dst_t[:, :], io[name].partition_broadcast(PT)).then_inc(s_small, 16)
            sp.dma_start(lnw[:, :, :], io["lnw"]).then_inc(s_small, 16)
            sp.dma_start(gate_raw[:, :, :], io["gate"]).then_inc(s_small, 16)

            def piece(i, p, src):
                if not isinstance(p, int) or p >= 2:
                    sp.wait_ge(w_lo, p - 1)
                sp.dma_start(raw[i][:, :], src).then_inc(s_w[i], 16)

            for p in range(P_EXP):
                name, q = ("gw", p) if p < P_IN else ("inw", p - P_IN) if p < P_OUT else ("outw", p - P_OUT)
                piece(p % 2, p, io[name][q])
            sp.wait_ge(w_lo, P_OUT + 1)
            sp.dma_start(bias9[:, :], io["bias9"]).then_inc(s_bias, 16)
            with sp.Fori(0, NE) as e:
                for q in range(4):
                    piece(q % 2, e * 4 + (P_EXP + q), io["expw"][ds(e, 1), q].rearrange("o p n -> (o p) n"))
            sp.wait_ge(s_final, NT)
            sp.dma_start(out.rearrange("(t p) n -> p t n", p=PT), x_sb[:, :, :]).then_inc(s_out, 16)
            sp.wait_ge(s_out, 16)
            if debug is not None:
                sp.wait_ge(at_ready, AHEAD + NWIN)
                sp.dma_start(debug["AT"][0], AT_h[:, :, :, :]).then_inc(s_dbg, 16)
                sp.dma_start(debug["AT"][1], AT_l[:, :, :, :]).then_inc(s_dbg, 16)
                sp.wait_ge(s_dbg, 32)
                sp.wait_ge(s_rng, 1)
                sp.dma_start(debug["rng"].rearrange("a (w k) -> a w k", k=4)[:, :, 0:3], rng[:, :].rearrange("a (w k) -> a w k", k=4)[:, :, 0:3]).then_inc(s_dbg, 16)
                sp.wait_ge(s_dbg, 48)

        @block.gpsimd
        def _(pool):
            g = nc.gpsimd
            g.memset(identf[:, :], 0.0).then_inc(s_pc, 1)
            g.memset(comb[:, :], 0.0).then_inc(s_pc, 1)
            g.memset(tri[:, :], 1.0).then_inc(s_pc, 1)
            g.memset(onesf[:, :], 1.0).then_inc(s_const, 1)
            pool.wait_ge(s_pc, 1)
            g.affine_select(out=identf[:, :], in_=identf[:, :], compare_op=ALU.not_equal, fill=1.0, base=0,
                            pattern=[[-1, 128]], channel_multiplier=1).then_inc(s_const, 1)
            pool.wait_ge(s_pc, 3)
            g.affine_select(out=tri[:, :], in_=tri[:, :], compare_op=ALU.is_gt, fill=0.0, base=0,
                            pattern=[[1, 128]], channel_multiplier=-1).then_inc(s_const, 1)
            g.iota(c_up[:, :], [[1, NCH]], base=1, channel_multiplier=0,
                   allow_small_or_imprecise_dtypes=True).then_inc(s_const, 1)
            g.iota(c_dn[:, :], [[-1, NCH]], base=NCH, channel_multiplier=0,
                   allow_small_or_imprecise_dtypes=True).then_inc(s_const, 1)
            g.iota(wlim[:, :], [[DW - 1, 2]], base=0, channel_multiplier=DW,
                   allow_small_or_imprecise_dtypes=True).then_inc(s_const, 1)
            g.iota(iota_s[:, :], [[1, SLP]], base=0, channel_multiplier=0,
                   allow_small_or_imprecise_dtypes=True).then_inc(s_const, 1)
            g.iota(iota_k[:, :], [[1, NWIN * KEYS]], base=0, channel_multiplier=0,
                   allow_small_or_imprecise_dtypes=True).then_inc(s_const, 1)
            g.iota(i4[:, :], [[-1, 4]], base=4, channel_multiplier=0,
                   allow_small_or_imprecise_dtypes=True).then_inc(s_const, 1)
            pool.wait_ge(s_pc, 2)
            cv = comb[:, :].rearrange("p (s m d) -> p m s d", s=2, m=2)
            n = 3
            for q in range(NQ):
                for s in range(2):
                    v = cv[:, 1 if q == NQ - 1 else 0, s, :]
                    last = g.affine_select(out=v, in_=v, compare_op=ALU.not_equal, fill=1.0,
                                           base=-(q * KEYS + s * DW), pattern=[[-1, DW]], channel_multiplier=1)
                    n += 1
                    last.then_inc(s_pc, 1)
                    pool.wait_ge(s_pc, n)
            g.tensor_copy(ident[:, :], identf[:, :]).then_inc(s_const, 1)
            def split(i, w):
                pool.wait_ge(t_copied, AHEAD + w + 1)
                src = T[i][:, :].rearrange("p (j m d) -> p j m d", m=2, d=DW)
                hi = AT_h[:, :, :, ds(w * DW, DW)]
                lo = AT_l[:, :, :, ds(w * DW, DW)]
                g.tensor_copy(hi, src).then_inc(at_hi, 1)
                pool.wait_ge(at_hi, w + 1)
                g.tensor_tensor(lo, src, hi, ALU.subtract).then_inc(at_ready, 1)
            g.memset(pmark[:, :], 0.0).then_inc(at_ready, AHEAD)
            split(0, 0)
            with pool.Fori(0, (NWIN - 1) // 2) as i:
                split(1, 2 * i + 1)
                split(0, 2 * i + 2)

        @block.vector
        def _(dve):
            v = nc.vector
            steps = [0]

            def link(ins):
                ins.then_inc(s_vc, 1)
                steps[0] += 1
                dve.wait_ge(s_vc, steps[0])


            def split_lo(i, p, dst):
                dve.wait_ge(w_hi, p + 1)
                v.scalar_tensor_tensor(dst[1], raw[i][:, :].rearrange("p (a n) -> p a n", a=dst[1].shape[1]), WS,
                                       dst[0], ALU.mult, ALU.subtract).then_inc(w_lo, 1)

            def rsqrt(vin, n, calls=[0]):
                vin.then_inc(s_sqin, 1)
                calls[0] += 1
                dve.wait_ge(s_sqin, calls[0])
                dve.wait_ge(s_sqout, calls[0])
                link(v.reciprocal(rx[:, 0:n], rw[:, 0:n]))
                link(v.tensor_tensor(rw[:, 0:n], rx[:, 0:n], rx[:, 0:n], ALU.mult))
                link(v.tensor_tensor(rw[:, 0:n], rw[:, 0:n], rv[:, 0:n], ALU.mult))
                link(v.tensor_scalar(rw[:, 0:n], rw[:, 0:n], -0.5, 1.5, ALU.mult, ALU.add))
                link(v.tensor_tensor(rx[:, 0:n], rx[:, 0:n], rw[:, 0:n], ALU.mult))

            def row_stats(src):
                for t in range(NT):
                    last = v.bn_stats(st6[:, t, :], src[:, t, :])
                link(last)
                for t in range(NT):
                    last = v.bn_aggr(mv[:, t, :], st6[:, t, :])
                link(last)
                rsqrt(v.tensor_scalar(rv[:, 0:NT], mv[:, :, 1], LNEPS, None, ALU.add), NT)

            dve.wait_ge(s_edge[1], 16)
            v.tensor_reduce(dmm[:, 0:3], dst_c[:, :, :], AX.X, ALU.min).then_inc(s_vc, 1)
            link(v.tensor_reduce(dmm[:, 3:6], dst_c[:, :, :], AX.X, ALU.max))
            steps[0] += 1
            dve.wait_ge(s_vc, steps[0])
            dve.wait_ge(s_const, 2)
            for k in range(6):
                v.tensor_scalar(diag[:, k, :], identf[0:CG, 0:CG], dmm[:, k:k + 1], None, ALU.mult).then_inc(s_dmm, 1)
            dve.wait_ge(s_edge[2], 16)
            dve.wait_ge(s_edge[0], 16)
            dlow, srcf, shi = scr0, scr1, slo_f
            v.tensor_single_scalar(dlow[:, :].bitcast(i32), e_dst[:, :], DW - 1, op=ALU.bitwise_and).then_inc(s_vc, 1)
            steps[0] += 1
            link(v.tensor_copy(srcf[:, :], e_src[:, :]))
            link(v.tensor_scalar(shi[:, :], srcf[:, :], float(SLO), None, ALU.is_ge))
            link(v.scalar_tensor_tensor(key_f[:, :], e_dst[:, :], 2.0, dlow[:, :].bitcast(i32), ALU.mult, ALU.subtract))
            link(v.scalar_tensor_tensor(key_f[:, :], shi[:, :], float(DW), key_f[:, :], ALU.mult, ALU.add))
            link(v.scalar_tensor_tensor(slo_f[:, :], shi[:, :], -float(SLO), srcf[:, :], ALU.mult, ALU.add))
            dve.wait_ge(s_bc, 2)
            dve.wait_ge(s_const, 6)
            link(v.tensor_scalar(hit[:, :], psX[1][0:NWIN, 0:NCH], wlim[:, 0:1], None, ALU.is_ge))
            link(v.scalar_tensor_tensor(hit[:, :], psX[0][0:NWIN, 0:NCH], wlim[:, 1:2], hit[:, :], ALU.is_le, ALU.mult))
            v.tensor_tensor(hit2[:, :], hit[:, :], c_dn[:, :], ALU.mult).then_inc(s_vc, 1)
            steps[0] += 1
            link(v.tensor_tensor(hit[:, :], hit[:, :], c_up[:, :], ALU.mult))
            v.tensor_reduce(rcol[:, 0:1], hit2[:, :], AX.X, ALU.max).then_inc(s_vc, 1)
            steps[0] += 1
            link(v.tensor_reduce(rcol[:, 1:2], hit[:, :], AX.X, ALU.max))
            link(v.tensor_scalar(rcol[:, 2:3], rcol[:, 0:1], -1.0, float(NCH), ALU.mult, ALU.add))
            link(v.tensor_scalar(rcol[:, 2:3], rcol[:, 2:3], float(NCH - 3), None, ALU.min))
            link(v.tensor_tensor(rcol[:, 3:4], rcol[:, 1:2], rcol[:, 2:3], ALU.subtract))
            v.tensor_scalar(rcol[:, 3:4], rcol[:, 3:4], 3.0, None, ALU.max).then_inc(s_rcol, 1)
            dve.wait_ge(s_edge[3], 16)
            link(v.memset(wq[:, :, NQ - 1], 1.0))
            link(v.tensor_copy(wq[:, :, 0], e_w[:, :]))
            link(v.tensor_tensor(scr0[:, :], e_w[:, :], wq[:, :, 0], ALU.subtract))
            link(v.tensor_copy(wq[:, :, 1], scr0[:, :]))
            link(v.tensor_tensor(scr0[:, :], scr0[:, :], wq[:, :, 1], ALU.subtract))
            link(v.tensor_copy(wq[:, :, 2], scr0[:, :]))
            dve.wait_ge(s_rrow, 1)
            v.tensor_copy(rng[0:1, :].rearrange("p (w k) -> p k w", k=4)[:, 0:3, :],
                          psX[0][0:1, 0:3 * NWIN].rearrange("p (k w) -> p k w", k=3)).then_inc(s_rng, 1)
            dve.wait_ge(s_rng, 1)
            for p in range(P_IN):
                wh = W[p // 2][:, 2 * (p % 2):2 * (p % 2) + 2, :, :]
                split_lo(p % 2, p, (wh[:, :, 0, :], wh[:, :, 1, :]))
            dve.wait_ge(s_small, 80)
            link(v.tensor_scalar(gate[:, :, 0, :], gate_raw[:, :, :], WS, None, ALU.mult))
            link(v.scalar_tensor_tensor(gate[:, :, 1, :], gate_raw[:, :, :], WS, gate[:, :, 0, :], ALU.mult,
                                        ALU.subtract))
            link(v.memset(ones16[:, :], 1.0))
            dve.wait_ge(s_const, 10)
            v.memset(scr1[:, 0:1], 0.0).then_inc(oh_free, NB)
            with dve.Fori(0, NWIN) as w:
                c0 = dve.value_load(rng[0:1, ds(4 * w, 1)], min_val=0, max_val=NCH - 3)
                cnt = dve.value_load(rng[0:1, ds(4 * w + 1, 1)], min_val=3, max_val=NCH)
                n0 = dve.value_load(rng[0:1, ds(4 * w + 2, 1)], min_val=0, max_val=NCH * NWIN)
                with dve.Fori(0, cnt) as k:
                    c = dve.snap(c0 + k).with_bounds(min_val=0, max_val=NCH - 1)
                    slot = dve.snap((n0 + k) % NB, min_val=0, max_val=NB - 1)
                    dve.wait_ge(oh_free, n0 + k + 1)
                    v.tensor_scalar(oh_src[:, ds(slot * SLP, SLP)], iota_s[:, :], slo_f[:, ds(c, 1)], None,
                                    ALU.is_equal)
                    v.scalar_tensor_tensor(
                        oh_key[:, ds(slot * 128, 128)].rearrange("p (q k) -> p q k", q=NQ),
                        iota_k[:, ds(w * KEYS, KEYS)].unsqueeze(1).to_broadcast([CH, NQ, KEYS]),
                        key_f[:, ds(c, 1)],
                        wq[:, ds(c, 1), :].rearrange("p o q -> p (o q)").unsqueeze(2).to_broadcast([CH, NQ, KEYS]),
                        ALU.is_equal, ALU.mult).then_inc(oh_ready, 1)

            dve.wait_ge(s_x, 16)
            row_stats(x_sb)
            link(v.tensor_copy(rs[:, :], rx[:, 0:NT]))
            dve.wait_ge(s_deg, 1)
            link(v.tensor_scalar(rx[:, :], psX[0][0:PT, 0:2 * NT], 1.0, None, ALU.add))
            link(v.tensor_scalar(pos[:, :], rx[:, :], 0.0, None, ALU.is_gt))
            link(v.tensor_tensor(rx[:, :], rx[:, :], pos[:, :], ALU.mult))
            link(v.tensor_scalar(rw[:, :], pos[:, :], -1.0, 1.0, ALU.mult, ALU.add))
            rsqrt(v.tensor_tensor(rv[:, :], rx[:, :], rw[:, :], ALU.add), 2 * NT)
            link(v.tensor_tensor(dis[:, :], rx[:, :], pos[:, :], ALU.mult))
            link(v.tensor_scalar(dsc[:, :], dis[:, :], 1.0 / WS, None, ALU.mult))
            link(v.tensor_tensor(rs[:, :], rs[:, :], dis[:, 0:NT], ALU.mult))

            def rows_lo(i, t, n):
                dve.wait_ge(xs_hi, n + 1)
                v.tensor_tensor(xs[:, ds(t, 1), 1, :].rearrange("p o n -> p (o n)"), xt[i][:, :],
                                xs[:, ds(t, 1), 0, :].rearrange("p o n -> p (o n)"), ALU.subtract).then_inc(xs_lo, 1)

            for t in range(NT):
                if t >= 2:
                    rows_lo(t % 2, t - 2, t - 2)
                    dve.wait_ge(xs_lo, t - 1)
                v.tensor_scalar(xt[t % 2][:, :], x_sb[:, t, :], mv[:, t, 0:1], rs[:, t:t + 1], ALU.subtract,
                                ALU.mult).then_inc(xt_ready, 1)
            rows_lo(0, NT - 2, NT - 2)
            rows_lo(1, NT - 1, NT - 1)

            def agg_low(layer):
                for c in range(CT):
                    ps = agg_ps[c % 2]
                    n = layer * CT + c
                    dve.wait_ge(agg_hi, n + 1)
                    v.tensor_tensor(aggT[:, c, 1, 0:1000].rearrange("p (a n) -> p a n", a=2),
                                    ps[0][:, :].rearrange("p (a n) -> p a n", a=2)[:, :, 0:500],
                                    aggT[:, c, 0, 0:1000].rearrange("p (a n) -> p a n", a=2), ALU.subtract)
                    v.tensor_tensor(aggT[:, c, 1, 1000:NODES], ps[1][:, 0:250], aggT[:, c, 0, 1000:NODES],
                                    ALU.subtract).then_inc(agg_lo, 1)

            agg_low(0)
            for t in range(NT):
                if t >= 2:
                    rows_lo(t % 2, t - 2, NT + t - 2)
                    dve.wait_ge(xs_lo, NT + t - 1)
                dve.wait_ge(lin_full, t + 1)
                v.scalar_tensor_tensor(xt[t % 2][:, :], psX[t % 2][0:PT, :], dsc[:, t:t + 1], b_bc[0][:, :], ALU.mult,
                                       ALU.add).then_inc(lin_read, 1)
                dve.wait_ge(lin_read, t + 1)
                v.tensor_scalar(xt[t % 2][:, :], xt[t % 2][:, :], 0.0, dis[:, NT + t:NT + t + 1], ALU.max,
                                ALU.mult).then_inc(xt_ready, 1)
            rows_lo(0, NT - 2, 2 * NT - 2)
            rows_lo(1, NT - 1, 2 * NT - 1)
            agg_low(1)
            def in_piece(p):
                k, q = divmod(p - P_IN, 8)
                c, half = divmod(q, 2)
                wh = inW[1 - k][:, c:c + 1, :, half * 1024:half * 1024 + 1024]
                return wh[:, :, 0, :], wh[:, :, 1, :]

            for t in range(NT):
                dve.wait_ge(lin_full, NT + t + 1)
                v.scalar_tensor_tensor(xt[t % 2][:, :], psX[t % 2][0:PT, :], dsc[:, NT + t:NT + t + 1], b_bc[1][:, :],
                                       ALU.mult, ALU.add).then_inc(lin_read, 1)
                dve.wait_ge(lin_read, NT + t + 1)
                v.tensor_tensor(x_sb[:, t, :], x_sb[:, t, :], xt[t % 2][:, :], ALU.add).then_inc(s_vc, 1)
                steps[0] += 1
                if t > 1:
                    split_lo(t % 2, P_IN + t - 2, in_piece(P_IN + t - 2))
            dve.wait_ge(s_vc, steps[0])

            row_stats(x_sb)
            for t in range(NT):
                last = v.tensor_scalar(zf[:, t, :], x_sb[:, t, :], mv[:, t, 0:1], rx[:, t:t + 1], ALU.subtract, ALU.mult)
            link(last)
            row_stats(zf)
            for t in range(NT):
                v.tensor_scalar(zf[:, t, :], zf[:, t, :], mv[:, t, 0:1], rx[:, t:t + 1], ALU.subtract,
                                ALU.mult).then_inc(zf_ready, 1)

            def flat_lo(t):
                dve.wait_ge(fl_hi, t + 1)
                v.tensor_tensor(flatT[:, :, 1, t * PT:(t + 1) * PT], vt[t % 2][:, :].rearrange("p (c n) -> p c n", c=CT),
                                flatT[:, :, 0, t * PT:(t + 1) * PT], ALU.subtract).then_inc(fl_lo, 1)

            for t in range(NT):
                if t >= 2:
                    flat_lo(t - 2)
                    dve.wait_ge(fl_lo, t - 1)
                dve.wait_ge(tr_full, t + 1)
                vv = vt[t % 2][:, :].rearrange("p (c n) -> p c n", c=CT)
                link(v.tensor_tensor(vv, psX[t % 2][:, 0:CT * PT].rearrange("p (c n) -> p c n", c=CT),
                                     lnw[:, 0, :].unsqueeze(2).to_broadcast([128, CT, PT]), ALU.mult))
                v.tensor_tensor(vv, vv, lnw[:, 1, :].unsqueeze(2).to_broadcast([128, CT, PT]), ALU.add).then_inc(
                    vt_ready, 1)
            flat_lo(NT - 2)
            flat_lo(NT - 1)
            for p in range(P_IN + 8, P_OUT):
                split_lo(p % 2, p, in_piece(p))

            gb = gb10[:, :].unsqueeze(1).to_broadcast([PT, NT, 10])
            es, pr, cand, oh = e4
            gs, mx, den, p2, t1 = r1

            def wide(a):
                return a[:, :].unsqueeze(2).to_broadcast([PT, NT, 4])

            i4b = i4[:, :].unsqueeze(1).to_broadcast([PT, NT, 4])
            dve.wait_ge(s_logit, 1)
            link(v.scalar_tensor_tensor(lg[:, :, :], psT[0][0:PT, 0:NT * 10].rearrange("p (t k) -> p t k", k=10),
                                        1.0 / WS, gb, ALU.mult, ALU.add))
            link(v.tensor_tensor(gs[:, :], lg[:, :, 1], lg[:, :, 0], ALU.is_gt))
            link(v.tensor_scalar(t1[:, :], gs[:, :], -1.0, 1.0, ALU.mult, ALU.add))
            link(v.tensor_tensor(es[:, :, :], lg[:, :, 2:6], wide(t1), ALU.mult))
            link(v.tensor_tensor(pr[:, :, :], lg[:, :, 6:10], wide(gs), ALU.mult))
            link(v.tensor_tensor(es[:, :, :], es[:, :, :], pr[:, :, :], ALU.add))
            link(v.tensor_reduce(mx[:, :], es[:, :, :], AX.X, ALU.max))
            v.tensor_tensor(es[:, :, :], es[:, :, :], wide(mx), ALU.subtract).then_inc(s_exin, 1)
            dve.wait_ge(s_exout, 1)
            link(v.tensor_reduce(den[:, :], es[:, :, :], AX.X, ALU.add))
            link(v.reciprocal(den[:, :], den[:, :]))
            link(v.tensor_tensor(pr[:, :, :], es[:, :, :], wide(den), ALU.mult))

            def top(best, onehot):
                link(v.tensor_reduce(best[:, :], pr[:, :, :], AX.X, ALU.max))
                link(v.tensor_tensor(cand[:, :, :], pr[:, :, :], wide(best), ALU.is_equal))
                link(v.tensor_tensor(cand[:, :, :], cand[:, :, :], i4b, ALU.mult))
                link(v.tensor_reduce(den[:, :], cand[:, :, :], AX.X, ALU.max))
                link(v.tensor_tensor(onehot, cand[:, :, :], wide(den), ALU.is_equal))

            top(mx, oh[:, :, :])
            link(v.scalar_tensor_tensor(pr[:, :, :], oh[:, :, :], -2.0, pr[:, :, :], ALU.mult, ALU.add))
            top(p2, es[:, :, :])
            link(v.scalar_tensor_tensor(den[:, :], mx[:, :], 1e-8, p2[:, :], ALU.add, ALU.add))
            link(v.reciprocal(den[:, :], den[:, :]))
            link(v.tensor_tensor(mx[:, :], mx[:, :], den[:, :], ALU.mult))
            link(v.tensor_tensor(p2[:, :], p2[:, :], den[:, :], ALU.mult))
            link(v.tensor_tensor(pr[:, :, :], oh[:, :, :], wide(mx), ALU.mult))
            link(v.tensor_tensor(cand[:, :, :], es[:, :, :], wide(p2), ALU.mult))
            link(v.tensor_tensor(pr[:, :, :], pr[:, :, :], cand[:, :, :], ALU.add))
            link(v.tensor_tensor(oh[:, :, :], oh[:, :, :], es[:, :, :], ALU.add))
            link(v.tensor_scalar(pr[:, :, :], pr[:, :, :], 1.0 / (WS * HS), None, ALU.mult))
            link(v.memset(cnt9[:, :, NE], 1.0))
            link(v.tensor_tensor(comb8[:, :, 0:4], pr[:, :, :], wide(t1), ALU.mult))
            link(v.tensor_tensor(comb8[:, :, 4:8], pr[:, :, :], wide(gs), ALU.mult))
            link(v.tensor_tensor(cnt9[:, :, 0:4], oh[:, :, :], wide(t1), ALU.mult))
            v.tensor_tensor(cnt9[:, :, 4:8], oh[:, :, :], wide(gs), ALU.mult).then_inc(s_route, 1)

            def hidden(k, g, n, jt):
                i = g % 2
                a0, width = SPANS[g % 3]
                dve.wait_ge(in_silu, n + 1)
                v.scalar_tensor_tensor(sl[i][:, 0:width], in_ps[i][:, 512:512 + width], HS / WS, sl[i][:, 0:width],
                                       ALU.mult, ALU.mult).then_inc(in_h, 1)
                dve.wait_ge(h_hi, n + 1)
                v.tensor_tensor(hT[k][:, ds(jt, 1), 1, a0:a0 + width].rearrange("p o n -> p (o n)"), sl[i][:, 0:width],
                                hT[k][:, ds(jt, 1), 0, a0:a0 + width].rearrange("p o n -> p (o n)"),
                                ALU.subtract).then_inc(h_lo, 1)

            v.memset(scr_mark[:, 0:1], 0.0).then_inc(in_h, AHEAD)
            v.memset(scr_mark[:, 1:2], 0.0).then_inc(h_lo, AHEAD)
            for k in (1, 0):
                with dve.Fori(0, 4) as jp:
                    for g in range(6):
                        hidden(k, g, jp * 6 + ((1 - k) * 24 + g), jp * 2 + g // 3)

            dve.wait_ge(s_cntT, 1)
            for b in range(3):
                last = v.tensor_copy(cntT[:, b * 4 * PT:min(NT, b * 4 + 4) * PT],
                                     (psT[0], psT[1], psX[0])[b][0:9, 0:min(4, NT - 4 * b) * PT])
            last.then_inc(s_cntTc, 1)

            def out_piece(slot, q):
                wh = outW[slot][:, 2 * q:2 * q + 2, :, :]
                return wh[:, :, 0, :], wh[:, :, 1, :]

            for q in range(4):
                split_lo(q % 2, P_OUT + q, out_piece(0, q))
            for e in range(2):
                for q in range(4):
                    split_lo(q % 2, P_EXP + 4 * e + q, out_piece(1 + e, q))
            for t in range(NT):
                dve.wait_ge(out_full, 2 * t + 1)
                v.scalar_tensor_tensor(x_sb[:, t, :], psX[0][0:PT, :], 1.0 / (WS * HS), x_sb[:, t, :], ALU.mult,
                                       ALU.add).then_inc(out_read, 1)
                dve.wait_ge(out_full, 2 * t + 2)
                dve.wait_ge(out_read, 2 * t + 1)
                v.tensor_tensor(x_sb[:, t, :], x_sb[:, t, :], psX[1][0:PT, :], ALU.add).then_inc(out_read, 1)
            def expert_tile(i, e, t, n):
                dve.wait_ge(out_full, 2 * NT + n + 1)
                dve.wait_ge(out_read, 2 * NT + n)
                xv = x_sb[:, ds(t, 1), :].rearrange("p o n -> p (o n)")
                return v.scalar_tensor_tensor(xv, psX[i][0:PT, :], comb8[:, ds(t, 1), ds(e, 1)].rearrange("p o n -> p (o n)"),
                                              xv, ALU.mult, ALU.add)
            def expert_pair(ep, more):
                for u in range(2):
                    with dve.Fori(0, NT // 2) as tp:
                        for i in range(2):
                            n = ep * (2 * NT) + tp * 2 + (u * NT + i)
                            expert_tile(i, ep * 2 + u, tp * 2 + i, n).then_inc(out_read, 1)
                    if more:
                        for q in range(4):
                            split_lo(q % 2, ep * 8 + (P_EXP + 8 + 4 * u + q), out_piece(1 + u, q))

            with dve.Fori(0, NE // 2 - 1) as ep:
                expert_pair(ep, True)
            expert_pair(NE // 2 - 1, False)
            dve.wait_ge(out_read, 2 * NT + NE * NT)
            v.memset(scr_mark[:, 2:3], 0.0).then_inc(s_final, NT)

        @block.tensor
        def _(pe):
            t = nc.tensor
            pe.wait_ge(s_dmm, 6)
            pe.wait_ge(s_const, 2)
            for k in range(6):
                last = t.matmul(psX[k // 3][0:NWIN, (k % 3) * CG:(k % 3 + 1) * CG], onesf[0:CG, 0:NWIN],
                                diag[:, k, :], start=True, stop=True)
                if k % 3 == 2:
                    last.then_inc(s_bc, 1)
            pe.wait_ge(s_rcol, 1)
            pe.wait_ge(s_const, 3)
            t.matmul(psX[0][0:1, 0:NWIN], rcol[:, 2:3], identf[0:NWIN, 0:NWIN], start=True, stop=True)
            t.matmul(psX[0][0:1, NWIN:2 * NWIN], rcol[:, 3:4], identf[0:NWIN, 0:NWIN], start=True, stop=True)
            t.matmul(psX[0][0:1, 2 * NWIN:3 * NWIN], rcol[:, 3:4], tri[0:NWIN, 0:NWIN], start=True,
                     stop=True).then_inc(s_rrow, 1)
            pe.wait_ge(s_rng, 1)
            pe.wait_ge(s_const, 10)

            def window(i, w):
                pe.wait_ge(r_copied, w + 1)
                cnt = pe.value_load(rng[0:1, ds(4 * w + 1, 1)], min_val=3, max_val=NCH)
                n0 = pe.value_load(rng[0:1, ds(4 * w + 2, 1)], min_val=0, max_val=NCH * NWIN)

                def step(k, start, stop):
                    slot = pe.snap((n0 + k) % NB, min_val=0, max_val=NB - 1)
                    pe.wait_ge(oh_ready, n0 + k + 1)
                    for h in range(2):
                        last = t.matmul(psR[i][:, h * 512:h * 512 + HW2], oh_key[:, ds(slot * 128, 128)],
                                        oh_src[:, ds(slot * SLP + h * HW2, HW2)], start=start, stop=stop)
                    last.then_inc(oh_free, 1)
                    return last
                step(0, True, False)
                with pe.Fori(1, cnt - 1) as k:
                    step(k, False, False)
                step(cnt - 1, False, True)
                t.matmul(psX[1][:, 0:1], ident[:, :], ident[:, 0:1], start=True, stop=True).then_inc(r_full, 1)

            def combine(i, w):
                pe.wait_ge(r_copied, AHEAD + w + 1)
                pe.wait_ge(t_copied, w + 1)
                for j in range(5):
                    last = t.matmul(psT[i][0:PT, j * 64:j * 64 + 64], R[i][:, j * PT:(j + 1) * PT], comb[:, :],
                                    start=True, stop=True)
                last.then_inc(t_full, 1)

            t.matmul(psX[1][:, 0:1], ident[:, :], ident[:, 0:1], start=True, stop=True).then_inc(t_full, AHEAD)
            window(0, 0)
            with pe.Fori(0, (NWIN - 1) // 2) as i:
                window(1, 2 * i + 1)
                combine(0, 2 * i)
                window(0, 2 * i + 2)
                combine(1, 2 * i + 1)
            combine(0, NWIN - 1)

            pe.wait_ge(at_ready, AHEAD + NWIN)
            with pe.Fori(0, NT) as j:
                for m in range(2):
                    for k in range(2 * NT):
                        A = (AT_h, AT_l)[k % 2]
                        last = t.matmul(psX[0][0:PT, ds(j + m * NT, 1)], A[:, k // 2, m, ds(j * PT, PT)],
                                        ones16[:, :], start=(k == 0), stop=(k == 2 * NT - 1))
            t.matmul(psX[1][:, 0:1], ident[:, :], ident[:, 0:1], start=True, stop=True).then_inc(s_deg, 1)

            def aggregate(layer):
                pe.wait_ge(xs_lo, (layer + 1) * NT)
                for c in range(CT):
                    n = layer * CT + c
                    if n >= 2:
                        pe.wait_ge(agg_lo, n - 1)
                    ps = agg_ps[c % 2]
                    outs = (ps[0][:, 0:500], ps[0][:, 512:1012], ps[1][:, 0:250])
                    for jj in range(NT):
                        j = (jj % 2) * 5 + jj // 2
                        for hl in range(2):
                            lhs = xs[:, j, hl, c * 128:(c + 1) * 128]
                            for A in ((AT_h, AT_l) if hl == 0 else (AT_h,)):
                                for b, (a0, width) in enumerate(SPANS):
                                    last = t.matmul(outs[b], lhs, A[:, jj, layer, a0:a0 + width],
                                                    start=(jj == 0 and hl == 0 and A is AT_h),
                                                    stop=(jj == NT - 1 and hl == 1))
                    for j in range(NT):
                        for hl in range(2):
                            last = t.matmul(outs[j // 4][:, (j % 4) * PT:(j % 4 + 1) * PT],
                                            xs[:, j, hl, c * 128:(c + 1) * 128], ident[0:PT, 0:PT], start=False,
                                            stop=False, skip_group_check=True)
                    last.then_inc(agg_full, 1)

            def linear(layer):
                pe.wait_ge(w_lo, P_IN)
                pe.wait_ge(agg_lo, (layer + 1) * CT)
                for tile in range(NT):
                    n = layer * NT + tile
                    if n >= 2:
                        pe.wait_ge(lin_read, n - 1)
                    k = 0
                    for c in range(CT):
                        for hl, wl in ((0, 0), (0, 1), (1, 0)):
                            last = t.matmul(psX[tile % 2][0:PT, :], aggT[:, c, hl, tile * PT:(tile + 1) * PT],
                                            W[layer][:, c, wl, :], start=(k == 0), stop=(k == 3 * CT - 1))
                            k += 1
                    last.then_inc(lin_full, 1)

            aggregate(0)
            linear(0)
            aggregate(1)
            linear(1)

            pe.wait_ge(lin_read, 2 * NT)
            for tile in range(NT):
                pe.wait_ge(zf_ready, tile + 1)
                if tile >= 2:
                    pe.wait_ge(vt_ready, tile - 1)
                for c in range(CT):
                    last = t.transpose(psX[tile % 2][:, c * PT:(c + 1) * PT], zf[:, tile, c * 128:(c + 1) * 128],
                                       identf[0:PT, 0:PT])
                last.then_inc(tr_full, 1)
            pe.wait_ge(fl_lo, NT)
            for tile in range(NT):
                k = 0
                for c in range(CT):
                    for hl, wl in ((0, 0), (0, 1), (1, 0)):
                        last = t.matmul(psT[0][0:PT, tile * 10:tile * 10 + 10],
                                        flatT[:, c, hl, tile * PT:(tile + 1) * PT], gate[:, c, wl, :],
                                        start=(k == 0), stop=(k == 3 * CT - 1))
                        k += 1
            last.then_inc(s_logit, 1)

            def hidden(k, g, n, jt):
                i = g % 2
                a0, width = SPANS[g % 3]
                pe.wait_ge(in_h, n + 1)
                for half in range(2):
                    m = 0
                    for c in range(CT):
                        for hl, wl in ((0, 0), (1, 0), (0, 1)):
                            last = t.matmul(in_ps[i][:, half * 512:half * 512 + width],
                                            inW[k][:, c, wl, ds(jt * 128 + half * HID, 128)],
                                            flatT[:, c, hl, a0:a0 + width], start=(m == 0), stop=(m == 3 * CT - 1))
                            m += 1
                last.then_inc(in_full, 1)

            for k in (1, 0):
                pe.wait_ge(w_lo, P_IN + 8 * (2 - k))
                with pe.Fori(0, 4) as jp:
                    for g in range(6):
                        n = jp * 6 + ((1 - k) * 24 + g)
                        hidden(k, g, n, jp * 2 + g // 3)
            pe.wait_ge(s_route, 1)
            pe.wait_ge(h_lo, AHEAD + 48)
            for tile in range(NT):
                last = t.transpose((psT[0], psT[1], psX[0])[tile // 4][0:9, (tile % 4) * PT:(tile % 4 + 1) * PT],
                                   cnt9[:, tile, :], identf[0:PT, 0:PT])
            last.then_inc(s_cntT, 1)
            pe.wait_ge(s_cntTc, 1)

            def project(k, ps, tile, slot):
                m = 0
                for j in range(8):
                    for hl, wl in ((0, 0), (0, 1), (1, 0)):
                        last = t.matmul(ps[0:PT, :], hT[k][:, j, hl, ds(tile * PT, PT)], outW[slot][:, j, wl, :],
                                        start=(m == 0), stop=(m == 23))
                        m += 1
                return last
            pe.wait_ge(w_lo, P_OUT + 4)
            pe.wait_ge(s_bias, 16)
            for tile in range(NT):
                if tile:
                    pe.wait_ge(out_read, 2 * tile - 1)
                project(0, psX[0], tile, 0).then_inc(out_full, 1)
                if tile:
                    pe.wait_ge(out_read, 2 * tile)
                t.matmul(psX[1][0:PT, :], cntT[:, tile * PT:(tile + 1) * PT], bias9[:, :], start=True,
                         stop=True).then_inc(out_full, 1)
            with pe.Fori(0, NE // 2) as ep:
                for u in range(2):
                    with pe.Fori(0, NT // 2) as tp:
                        for i in range(2):
                            pe.wait_ge(w_lo, ep * 8 + (P_EXP + 4 * u + 4))
                            n = ep * (2 * NT) + tp * 2 + (u * NT + i)
                            pe.wait_ge(out_read, n + (2 * NT - 1))
                            project(1, psX[i], tp * 2 + i, 1 + u).then_inc(out_full, 1)

        @block.scalar
        def _(act):
            a = nc.scalar

            def split_hi(i, p, dst):
                act.wait_ge(s_w[i], (p // 2 + 1) * 16)
                a.activation(dst, raw[i][:, :].rearrange("p (a n) -> p a n", a=dst.shape[1]), ACT.Copy,
                             scale=WS).then_inc(w_hi, 1)

            for p in range(P_IN):
                split_hi(p % 2, p, W[p // 2][:, 2 * (p % 2):2 * (p % 2) + 2, 0, :])

            def evac_r(i, w):
                act.wait_ge(r_full, w + 1)
                act.wait_ge(t_full, w + 1)
                a.activation(R[i][:, :].rearrange("p (h s) -> p h s", h=2),
                             psR[i][:, :].rearrange("p (h s) -> p h s", h=2)[:, :, 0:HW2],
                             ACT.Copy).then_inc(r_copied, 1)

            def evac_t(i, w):
                act.wait_ge(t_full, AHEAD + w + 1)
                act.wait_ge(at_ready, w + 1)
                a.activation(T[i][:, :], psT[i][0:PT, 0:320], ACT.Copy).then_inc(t_copied, 1)

            act.wait_ge(s_const, 10)
            a.activation(amark[:, 0:1], ident[0:1, 0:1], ACT.Copy).then_inc(t_copied, AHEAD)
            a.activation(amark[:, 1:2], ident[0:1, 0:1], ACT.Copy).then_inc(r_copied, AHEAD)
            evac_r(0, 0)
            with act.Fori(0, (NWIN - 1) // 2) as i:
                evac_r(1, 2 * i + 1)
                evac_t(0, 2 * i)
                evac_r(0, 2 * i + 2)
                evac_t(1, 2 * i + 1)
            evac_t(0, NWIN - 1)

            def sqrt(n, calls):
                act.wait_ge(s_sqin, calls)
                a.activation(rw[:, 0:n], rv[:, 0:n], ACT.Sqrt).then_inc(s_sqout, 1)

            def rows_hi(layer):
                for t in range(NT):
                    act.wait_ge(xt_ready, layer * NT + t + 1)
                    a.activation(xs[:, t, 0, :], xt[t % 2][:, :], ACT.Copy).then_inc(xs_hi, 1)

            def agg_high(layer):
                for c in range(CT):
                    ps = agg_ps[c % 2]
                    act.wait_ge(agg_full, layer * CT + c + 1)
                    a.activation(aggT[:, c, 0, 0:1000].rearrange("p (a n) -> p a n", a=2),
                                 ps[0][:, :].rearrange("p (a n) -> p a n", a=2)[:, :, 0:500], ACT.Copy)
                    a.activation(aggT[:, c, 0, 1000:NODES], ps[1][:, 0:250], ACT.Copy).then_inc(agg_hi, 1)

            sqrt(NT, 1)
            sqrt(2 * NT, 2)
            rows_hi(0)
            agg_high(0)
            rows_hi(1)
            agg_high(1)
            for p in range(P_IN, P_IN + 8):
                k, q = divmod(p - P_IN, 8)
                split_hi(p % 2, p, inW[1 - k][:, q // 2:q // 2 + 1, 0, (q % 2) * 1024:(q % 2) * 1024 + 1024])
            sqrt(NT, 3)
            sqrt(NT, 4)
            for t in range(NT):
                act.wait_ge(vt_ready, t + 1)
                a.activation(flatT[:, :, 0, t * PT:(t + 1) * PT], vt[t % 2][:, :].rearrange("p (c n) -> p c n", c=CT),
                             ACT.Copy).then_inc(fl_hi, 1)
            for p in range(P_IN + 8, P_OUT):
                k, q = divmod(p - P_IN, 8)
                split_hi(p % 2, p, inW[1 - k][:, q // 2:q // 2 + 1, 0, (q % 2) * 1024:(q % 2) * 1024 + 1024])
            act.wait_ge(s_exin, 1)
            a.activation(e4[0][:, :, :], e4[0][:, :, :], ACT.Exp).then_inc(s_exout, 1)

            def hidden(k, g, n, jt):
                i = g % 2
                a0, width = SPANS[g % 3]
                act.wait_ge(in_full, n + 1)
                act.wait_ge(h_lo, n + 1)
                a.activation(sl[i][:, 0:width], in_ps[i][:, 0:width], ACT.Silu, scale=1.0 / WS).then_inc(in_silu, 1)
                act.wait_ge(in_h, AHEAD + n + 1)
                a.activation(hT[k][:, ds(jt, 1), 0, a0:a0 + width].rearrange("p o n -> p (o n)"), sl[i][:, 0:width],
                             ACT.Copy).then_inc(h_hi, 1)

            for k in (1, 0):
                with act.Fori(0, 4) as jp:
                    for g in range(6):
                        hidden(k, g, jp * 6 + ((1 - k) * 24 + g), jp * 2 + g // 3)
            for q in range(4):
                split_hi(q % 2, P_OUT + q, outW[0][:, 2 * q:2 * q + 2, 0, :])
            for e in range(2):
                for q in range(4):
                    split_hi(q % 2, P_EXP + 4 * e + q, outW[1 + e][:, 2 * q:2 * q + 2, 0, :])
            with act.Fori(0, NE // 2 - 1) as ep:
                for u in range(2):
                    act.wait_ge(out_full, ep * (2 * NT) + (2 * NT + (u + 1) * NT))
                    for q in range(4):
                        act.wait_ge(s_w[q % 2], ep * 64 + ((P_EXP + 8 + 4 * u + q) // 2 + 1) * 16)
                        a.activation(outW[1 + u][:, 2 * q:2 * q + 2, 0, :], raw[q % 2][:, :].rearrange("p (a n) -> p a n", a=2),
                                     ACT.Copy, scale=WS).then_inc(w_hi, 1)


_OUT_ROWS = NODES
DEBUG = False


def kernel(**inputs):
    import numpy as np
    import concourse.bacc as _bacc
    from concourse import mybir as _mybir
    from concourse.bass_utils import run_bass_kernel_spmd as _run

    nc = _bacc.Bacc("TRN2", target_bir_lowering=False, num_devices=1)
    arrays, io = {}, {}

    def give(name, a):
        a = np.ascontiguousarray(a)
        arrays[f"in_{name}"] = a
        io[name] = nc.dram_tensor(f"in_{name}", a.shape, _mybir.dt.from_np(a.dtype), kind="ExternalInput").ap()

    def padded(a, fill):
        return np.concatenate([a, np.full(NCH * CH - EDGES, fill, a.dtype)])

    src, dst = padded(inputs["src"], 4000), padded(inputs["dst"], 2 * NODES)
    give("e_src", src.reshape(NCH, CH).T)
    give("e_dst", dst.reshape(NCH, CH).T)
    give("e_w", padded(inputs["edge_weight"], 0).reshape(NCH, CH).T)
    give("dst_c", dst.reshape(3, CG, CH).transpose(1, 0, 2))
    give("x", inputs["x"].reshape(NT, PT, DIM).transpose(1, 0, 2))
    give("b1", inputs["L0_gnn_b1"])
    give("b2", inputs["L0_gnn_b2"])
    give("gb10", np.concatenate([inputs["L0_ffn_group_bias"], inputs["L0_ffn_expert_bias"]]))
    give("lnw", np.stack([inputs["L0_ffn_ln_scale"], inputs["L0_ffn_ln_bias"]]).reshape(2, CT, 128).transpose(2, 0, 1))
    gates = np.concatenate([inputs["L0_ffn_group_gate_w"], inputs["L0_ffn_expert_gate_w"]])
    give("gate", gates.T.reshape(CT, 128, 10).transpose(1, 0, 2))
    give("bias9", np.concatenate([inputs["L0_ffn_expert_out_bias"], inputs["L0_ffn_shared_out_b"][None]]))
    give("gw", np.stack([inputs[f"L0_gnn_W{i}"].reshape(2, 2, 128, DIM).transpose(0, 2, 1, 3).reshape(2, 128, 1024)
                         for i in (1, 2)]).reshape(4, 128, 1024))
    give("inw", np.stack([inputs[f"L0_ffn_{n}_in_w"].T.reshape(CT, 128, 2, 1024).transpose(0, 2, 1, 3)
                          for n in ("expert", "shared")]).reshape(16, 128, 1024))
    give("outw", inputs["L0_ffn_shared_out_w"].T.reshape(4, 2, 128, DIM).transpose(0, 2, 1, 3).reshape(4, 128, 1024))
    give("expw", inputs["L0_ffn_expert_out_weight"].transpose(0, 2, 1).reshape(NE, 4, 2, 128, DIM)
         .transpose(0, 1, 3, 2, 4).reshape(NE, 4, 128, 1024))
    out = nc.dram_tensor("out_0_dram", (_OUT_ROWS, DIM), _mybir.dt.float32, kind="ExternalOutput").ap()
    dbg = None
    if DEBUG:
        at = nc.dram_tensor("dbg_AT", (2, PT, NT, 2, DPAD), _mybir.dt.float16, kind="ExternalOutput").ap()
        rg = nc.dram_tensor("dbg_rng", (1, NWIN * 4), _mybir.dt.int32, kind="ExternalOutput").ap()
        dbg = {"AT": at, "rng": rg}
    gnn_ffn_kernel(nc, io, out, dbg)
    r = _run(nc, [arrays], core_ids=[0])
    return r.results[0]["out_0_dram"]
```

```python
import concourse.bass as bass
from concourse import mybir
from contextlib import ExitStack

NODES, DIM, EDGES = 1250, 512, 41250
PT = 125
NT = NODES // PT
CT = DIM // 128
CH = 128
NCH = 324
CG = NCH // 3
GC = 3
NG = NCH // GC
NCP = NCH + GC
DW = 16
NWIN = -(-NODES // DW)
DPAD = 1272
SLO = NODES // 2
HW2 = 313
SLP = 2 * HW2
KEYS = 2 * DW
NQ = 4
AHEAD = 2
NOH = 9
NKR = 3
NB = 4
HID = 1024
NE = 8
WS = 64.0
HS = 16.0
LNEPS = 1e-5


def gnn_ffn_kernel(nc, io, out, debug=None):
    f32, i32, i16 = mybir.dt.float32, mybir.dt.int32, mybir.dt.int16
    bf16, f16 = mybir.dt.bfloat16, mybir.dt.float16
    ALU = mybir.AluOpType
    ACT = mybir.ActivationFunctionType
    AX = mybir.AxisListType
    ds = bass.ds

    ctx = ExitStack()
    with ctx:
        size_of = {f32: 4, i32: 4, i16: 2, bf16: 2, f16: 2}
        base = 16512

        class Region:
            def __init__(self, start, size):
                self.at, self.end, self.start = start, start + size, start

            def __call__(self, name, shape, dt):
                n = size_of[dt]
                for s in shape[1:]:
                    n *= s
                t = nc.alloc_sbuf_tensor_at(name, shape, dt, offset=self.at)
                self.at += -(-n // 32) * 32
                assert self.at <= self.end, (name, self.at - self.start, self.end - self.start)
                return t

        def region(size):
            nonlocal base
            r = Region(base, size)
            base += size
            return r

        keep = region(20480 + 8704 + 896)
        slots = region(NE * 16384)
        share = region(40960)
        stage = region(212832 - base + 16512)

        def pb(name, banks=1, dt=f32):
            n = 512 * banks if dt == f32 else 1024 * banks
            return ctx.enter_context(nc.psum_tensor(name, [128, n], dt))

        def sem(name):
            return ctx.enter_context(nc.semaphore(name))

        x_sb = keep("x_sb", [PT, NT, DIM], f32)
        identf = keep("identf", [128, 128], f32)
        ident = keep("ident", [128, 128], f16)
        onesf = keep("onesf", [CG, NWIN], f32)

        AT_h = nc.alloc_sbuf_tensor_at("AT_h", [PT, NT, 2, DPAD], f16, offset=slots.start)
        AT_l = nc.alloc_sbuf_tensor_at("AT_l", [PT, NT, 2, DPAD], f16, offset=slots.start + NT * 2 * DPAD * 2)
        slots.at += NT * 2 * DPAD * 2 * 2
        prep = Region(share.at, 13000)
        e_src = prep("e_src", [CH, NCP], i32)
        e_dst = prep("e_dst", [CH, NCP], i32)
        e_w = prep("e_w", [CH, NCP], f32)
        scr0 = prep("scr0", [CH, NCP], f32)
        scr1 = prep("scr1", [CH, NCP], f32)
        c_up = prep("c_up", [NWIN, NCH], f32)
        c_dn = prep("c_dn", [NWIN, NCH], f32)
        oh_src = share("oh_src", [CH, NOH * SLP], bf16)
        share.at = max(share.at, prep.at)
        oh_key = share("oh_key", [CH, NKR * 4 * 128], bf16)
        eq = share("eq", [CH, NKR, 4, KEYS], bf16)
        key_g = share("key_g", [CH, NG, 4], f32)
        slo_f = share("slo_f", [CH, NCP], f32)
        key_f = share("key_f", [CH, NCP], f32)
        wq = share("wq", [CH, NCP, NQ], bf16)
        iota_s = share("iota_s", [CH, SLP], i16)
        iota_k = share("iota_k", [CH, NWIN * KEYS], i16)
        R = [share(f"R{i}", [128, SLP], f32) for i in range(2)]
        prep3 = Region(slots.at, 2560)
        step_d = prep3("step_d", [CG, 3, CH], f32)
        ends_f = prep3("ends_f", [1, 2, NG], f32)
        T = [slots(f"T{i}", [PT, 5 * 2 * KEYS], f32) for i in range(2)]
        comb = slots("comb", [128, 2 * KEYS], f32)
        tri = slots("tri", [128, 128], f32)
        dmm = slots("dmm", [CG, 6], f32)
        dst_c = slots("dst_c", [CG, 3, CH + 1], i32)
        viol = slots("viol", [CG, 2], f32)
        vrow = slots("vrow", [1, 4], f32)
        ones1 = slots("ones1", [1, 128], f32)
        diag = slots("diag", [CG, 6, CG], f32)
        prep2 = Region(slots.at, 4096)
        hit = prep2("hit", [NWIN, NCH], f32)
        hit2 = prep2("hit2", [NWIN, NCH], f32)
        ends_i = prep2("ends_i", [1, 2, NG], i32)
        base_f = prep2("base_f", [1, NG + 1], f32)
        xt = [slots(f"xt{i}", [PT, DIM], f32) for i in range(2)]
        wlim = slots("wlim", [NWIN, 2], f32)
        rcol = slots("rcol", [NWIN, 4], f32)
        marks = keep("marks", [1, 8], f32)
        pmark = keep("pmark", [1, 1], f32)
        amark = keep("amark", [1, 2], f32)
        base_i = keep("base_i", [1, NG + 4], i32)
        flag_i = keep("flag_i", [1, 1], i32)
        scr_mark = keep("scr_mark", [1, 4], f32)
        rng = keep("rng", [1, NWIN * 4], i32)

        g_share = Region(share.start, 40960)
        xs = g_share("xs", [PT, NT, 2, DIM], f16)
        aggT = g_share("aggT", [128, CT, 2, NODES], f16)
        W = [slots(f"W{i}", [128, CT, 2, DIM], f16) for i in range(2)]
        raw = [stage(f"raw{i}", [128, 1024], f32) for i in range(2)]
        f_share = Region(share.start, 40960)
        zf = f_share("zf", [PT, NT, DIM], f32)
        vt = [f_share(f"vt{i}", [128, CT * PT], f32) for i in range(2)]
        h_share = Region(share.start, 40960)
        hT = [h_share("hT_shared", [128, 8, 2, NODES], f16)]
        f_slots = Region(slots.start, NE * 16384)
        hT.append(f_slots("hT_expert", [128, 8, 2, NODES], f16))
        flatT = f_slots("flatT", [128, CT, 2, NODES], f16)
        o_slots = Region(f_slots.at, 65536)
        inW = [f_slots(f"inW{i}", [128, CT, 2, 2 * HID], f16) for i in (1, 0)][::-1]
        outW = [o_slots(f"outW{i}", [128, 8, 2, DIM], f16) for i in range(3)]
        sl = [f_slots(f"sl{i}", [128, 500], f32) for i in range(2)]
        b_bc = [keep(f"b_bc{i}", [PT, DIM], f32) for i in range(2)]
        lnw = keep("lnw", [128, 2, CT], f32)
        gate_raw = stage("gate_raw", [128, CT, 10], f32)
        gate = stage("gate", [128, CT, 2, 10], f16)
        gb10 = stage("gb10", [PT, 10], f32)
        st6 = stage("st6", [PT, NT, 6], f32)
        mv = stage("mv", [PT, NT, 2], f32)
        rs = stage("rs", [PT, NT], f32)
        rv = stage("rv", [PT, 2 * NT], f32)
        rw = stage("rw", [PT, 2 * NT], f32)
        rx = stage("rx", [PT, 2 * NT], f32)
        pos = stage("pos", [PT, 2 * NT], f32)
        dis = stage("dis", [PT, 2 * NT], f32)
        dsc = stage("dsc", [PT, 2 * NT], f32)
        ones16 = stage("ones16", [PT, 1], f16)
        cnt9 = keep("cnt9", [PT, NT, 9], f32)
        c_slots = Region(f_slots.start + 40000, 20000)
        cntT = c_slots("cntT", [9, NODES], f32)
        bias9 = c_slots("bias9", [9, DIM], f32)
        comb8 = keep("comb8", [PT, NT, NE], f32)
        lg = keep("lg", [PT, NT, 10], f32)
        e4 = [keep(f"e4_{i}", [PT, NT, 4], f32) for i in range(4)]
        r1 = [keep(f"r1_{i}", [PT, NT], f32) for i in range(5)]
        i4 = keep("i4", [PT, 4], f32)

        psR = [pb(f"psR{i}", 2) for i in range(2)]
        psT = [pb(f"psT{i}") for i in range(2)]
        psX = [pb(f"psX{i}") for i in range(2)]

        s_edge = [sem(f"s_edge{i}") for i in range(5)]
        s_const = sem("s_const")
        s_pc = sem("s_pc")
        s_vc = sem("s_vc")
        s_dmm = sem("s_dmm")
        s_bc = sem("s_bc")
        s_rcol = sem("s_rcol")
        s_rrow = sem("s_rrow")
        s_rng = sem("s_rng")
        oh_ready = sem("oh_ready")
        oh_free = sem("oh_free")
        r_full = sem("r_full")
        r_copied = sem("r_copied")
        t_full = sem("t_full")
        t_copied = sem("t_copied")
        at_hi = sem("at_hi")
        at_ready = sem("at_ready")
        s_viol = sem("s_viol")
        g_start = sem("g_start")
        s_base = sem("s_base")
        s_bb = sem("s_bb")
        s_flag = sem("s_flag")
        g_oh = sem("g_oh")
        g_eq = sem("g_eq")
        g_q = sem("g_q")
        g_sum = sem("g_sum")
        g_rc = sem("g_rc")
        g_comb = sem("g_comb")
        g_hi = sem("g_hi")
        g_lo = sem("g_lo")
        g_zero = sem("g_zero")
        s_dbg = sem("s_dbg")
        s_x = sem("s_x")
        s_bias = sem("s_bias")
        s_small = sem("s_small")
        s_w = [sem(f"s_w{i}") for i in range(2)]
        w_hi = sem("w_hi")
        w_lo = sem("w_lo_done")
        s_sqin = sem("s_sqin")
        s_sqout = sem("s_sqout")
        s_deg = sem("s_deg")
        xt_ready = sem("xt_ready")
        xs_hi = sem("xs_hi")
        xs_lo = sem("xs_lo")
        agg_full = sem("agg_full")
        agg_hi = sem("agg_hi")
        agg_lo = sem("agg_lo")
        lin_full = sem("lin_full")
        lin_read = sem("lin_read")
        zf_ready = sem("zf_ready")
        tr_full = sem("tr_full")
        vt_ready = sem("vt_ready")
        fl_hi = sem("fl_hi")
        fl_lo = sem("fl_lo")
        s_logit = sem("s_logit")
        s_lg = sem("s_lg")
        s_exin = sem("s_exin")
        s_exout = sem("s_exout")
        s_route = sem("s_route")
        in_full = sem("in_full")
        in_silu = sem("in_silu")
        in_h = sem("in_h")
        h_hi = sem("h_hi")
        h_lo = sem("h_lo")
        s_cntT = sem("s_cntT")
        s_cntTc = sem("s_cntTc")
        out_full = sem("out_full")
        out_read = sem("out_read")
        s_final = sem("s_final")
        s_out = sem("s_out")

        agg_ps = [(psR[i], psT[i]) for i in range(2)]
        in_ps = [psR[i] for i in range(2)]
        SPANS = [(0, 500), (500, 500), (1000, 250)]
        P_W, P_IN, P_OUT, P_EXP = 0, 4, 20, 24

        block = ctx.enter_context(nc.Block())

        @block.sync
        def _(sp):
            sp.dma_start(e_dst[:, :], io["e_dst"]).then_inc(s_edge[0], 16)
            sp.dma_start(dst_c[:, :, :], io["dst_c"]).then_inc(s_edge[1], 16)
            sp.dma_start(ends_i[:, :, :], io["ends"]).then_inc(s_edge[4], 16)
            sp.dma_start(e_src[:, :], io["e_src"]).then_inc(s_edge[2], 16)
            sp.dma_start(e_w[:, :], io["e_w"]).then_inc(s_edge[3], 16)
            sp.dma_start(x_sb[:, :, :], io["x"]).then_inc(s_x, 16)
            for dst_t, name in ((b_bc[0], "b1"), (b_bc[1], "b2"), (gb10, "gb10")):
                sp.dma_start(dst_t[:, :], io[name].partition_broadcast(PT)).then_inc(s_small, 16)
            sp.dma_start(lnw[:, :, :], io["lnw"]).then_inc(s_small, 16)
            sp.dma_start(gate_raw[:, :, :], io["gate"]).then_inc(s_small, 16)

            def piece(i, p, src):
                if not isinstance(p, int) or p >= 2:
                    sp.wait_ge(w_lo, p - 1)
                sp.dma_start(raw[i][:, :], src).then_inc(s_w[i], 16)

            for p in range(P_EXP):
                name, q = ("gw", p) if p < P_IN else ("inw", p - P_IN) if p < P_OUT else ("outw", p - P_OUT)
                piece(p % 2, p, io[name][q])
            sp.wait_ge(w_lo, P_OUT + 1)
            sp.dma_start(bias9[:, :], io["bias9"]).then_inc(s_bias, 16)
            with sp.Fori(0, NE) as e:
                for q in range(4):
                    piece(q % 2, e * 4 + (P_EXP + q), io["expw"][ds(e, 1), q].rearrange("o p n -> (o p) n"))
            sp.wait_ge(s_final, NT)
            sp.dma_start(out.rearrange("(t p) n -> p t n", p=PT), x_sb[:, :, :]).then_inc(s_out, 16)
            sp.wait_ge(s_out, 16)
            if debug is not None:
                sp.wait_ge(at_ready, AHEAD + NWIN)
                sp.dma_start(debug["AT"][0], AT_h[:, :, :, :]).then_inc(s_dbg, 16)
                sp.dma_start(debug["AT"][1], AT_l[:, :, :, :]).then_inc(s_dbg, 16)
                sp.wait_ge(s_dbg, 32)
                sp.wait_ge(s_rng, 1)
                sp.dma_start(debug["rng"].rearrange("a (w k) -> a w k", k=4)[:, :, 0:3], rng[:, :].rearrange("a (w k) -> a w k", k=4)[:, :, 0:3]).then_inc(s_dbg, 16)
                sp.wait_ge(s_dbg, 48)

        @block.gpsimd
        def _(pool):
            g = nc.gpsimd
            g.memset(identf[:, :], 0.0).then_inc(s_pc, 1)
            g.memset(comb[:, :], 0.0).then_inc(s_pc, 1)
            g.memset(tri[:, :], 1.0).then_inc(s_pc, 1)
            g.memset(onesf[:, :], 1.0).then_inc(s_const, 1)
            pool.wait_ge(s_pc, 1)
            g.affine_select(out=identf[:, :], in_=identf[:, :], compare_op=ALU.not_equal, fill=1.0, base=0,
                            pattern=[[-1, 128]], channel_multiplier=1).then_inc(s_const, 1)
            pool.wait_ge(s_pc, 3)
            g.affine_select(out=tri[:, :], in_=tri[:, :], compare_op=ALU.is_gt, fill=0.0, base=0,
                            pattern=[[1, 128]], channel_multiplier=-1).then_inc(s_const, 1)
            g.iota(c_up[:, :], [[1, NCH]], base=1, channel_multiplier=0,
                   allow_small_or_imprecise_dtypes=True).then_inc(s_const, 1)
            g.iota(c_dn[:, :], [[-1, NCH]], base=NCH, channel_multiplier=0,
                   allow_small_or_imprecise_dtypes=True).then_inc(s_const, 1)
            g.iota(wlim[:, :], [[DW - 1, 2]], base=0, channel_multiplier=DW,
                   allow_small_or_imprecise_dtypes=True).then_inc(s_const, 1)
            g.iota(iota_s[:, :], [[1, SLP]], base=0, channel_multiplier=0,
                   allow_small_or_imprecise_dtypes=True).then_inc(s_const, 1)
            g.iota(iota_k[:, :], [[1, NWIN * KEYS]], base=0, channel_multiplier=0,
                   allow_small_or_imprecise_dtypes=True).then_inc(s_const, 1)
            g.iota(i4[:, :], [[-1, 4]], base=4, channel_multiplier=0,
                   allow_small_or_imprecise_dtypes=True).then_inc(s_const, 1)
            pool.wait_ge(s_pc, 2)
            cv = comb[:, :].rearrange("p (s m d) -> p m s d", s=2, m=2)
            n = 3
            for q in range(NQ):
                for s in range(2):
                    v = cv[:, 1 if q == NQ - 1 else 0, s, :]
                    last = g.affine_select(out=v, in_=v, compare_op=ALU.not_equal, fill=1.0,
                                           base=-(q * KEYS + s * DW), pattern=[[-1, DW]], channel_multiplier=1)
                    n += 1
                    last.then_inc(s_pc, 1)
                    pool.wait_ge(s_pc, n)
            g.tensor_copy(ident[:, :], identf[:, :]).then_inc(s_const, 1)
            pool.wait_ge(s_flag, 1)
            fast = pool.value_load(flag_i[0:1, 0:1])
            with pool.If(fast > 0):
                g.memset(AT_l[:, :, 1, :], 0.0).then_inc(g_zero, 1)

                def keys(u, n):
                    slot = u % NKR
                    pool.wait_ge(g_eq, n + 1)
                    pool.wait_ge(g_sum, n + 1)
                    g.tensor_tensor(oh_key[:, slot * 512:(slot + 1) * 512].rearrange("p (c q k) -> p c q k", c=4, q=NQ),
                                    eq[:, slot].unsqueeze(2).to_broadcast([CH, 4, NQ, KEYS]),
                                    wq[:, ds(n * GC, 4), :].unsqueeze(3).to_broadcast([CH, 4, NQ, KEYS]),
                                    ALU.mult).then_inc(g_q, 1)
                with pool.Fori(0, NG // 6) as i:
                    for u in range(6):
                        keys(u, i * 6 + u)
            with pool.Else():
                def split(i, w):
                    pool.wait_ge(t_copied, AHEAD + w + 1)
                    src = T[i][:, :].rearrange("p (j m d) -> p j m d", m=2, d=DW)
                    hi = AT_h[:, :, :, ds(w * DW, DW)]
                    lo = AT_l[:, :, :, ds(w * DW, DW)]
                    g.tensor_copy(hi, src).then_inc(at_hi, 1)
                    pool.wait_ge(at_hi, w + 1)
                    g.tensor_tensor(lo, src, hi, ALU.subtract).then_inc(at_ready, 1)
                g.memset(pmark[:, :], 0.0).then_inc(at_ready, AHEAD)
                split(0, 0)
                with pool.Fori(0, (NWIN - 1) // 2) as i:
                    split(1, 2 * i + 1)
                    split(0, 2 * i + 2)

        @block.vector
        def _(dve):
            v = nc.vector
            steps = [0]

            def link(ins):
                ins.then_inc(s_vc, 1)
                steps[0] += 1
                dve.wait_ge(s_vc, steps[0])


            def split_lo(i, p, dst):
                dve.wait_ge(w_hi, p + 1)
                v.scalar_tensor_tensor(dst[1], raw[i][:, :].rearrange("p (a n) -> p a n", a=dst[1].shape[1]), WS,
                                       dst[0], ALU.mult, ALU.subtract).then_inc(w_lo, 1)

            def rsqrt(vin, n, calls=[0]):
                vin.then_inc(s_sqin, 1)
                calls[0] += 1
                dve.wait_ge(s_sqin, calls[0])
                dve.wait_ge(s_sqout, calls[0])
                link(v.reciprocal(rx[:, 0:n], rw[:, 0:n]))
                link(v.tensor_tensor(rw[:, 0:n], rx[:, 0:n], rx[:, 0:n], ALU.mult))
                link(v.tensor_tensor(rw[:, 0:n], rw[:, 0:n], rv[:, 0:n], ALU.mult))
                link(v.tensor_scalar(rw[:, 0:n], rw[:, 0:n], -0.5, 1.5, ALU.mult, ALU.add))
                link(v.tensor_tensor(rx[:, 0:n], rx[:, 0:n], rw[:, 0:n], ALU.mult))

            def row_stats(src):
                for t in range(NT):
                    last = v.bn_stats(st6[:, t, :], src[:, t, :])
                link(last)
                for t in range(NT):
                    last = v.bn_aggr(mv[:, t, :], st6[:, t, :])
                link(last)
                rsqrt(v.tensor_scalar(rv[:, 0:NT], mv[:, :, 1], LNEPS, None, ALU.add), NT)

            dve.wait_ge(s_edge[1], 16)
            v.tensor_reduce(dmm[:, 0:3], dst_c[:, :, 0:CH], AX.X, ALU.min).then_inc(s_vc, 1)
            link(v.tensor_reduce(dmm[:, 3:6], dst_c[:, :, 0:CH], AX.X, ALU.max))
            steps[0] += 1
            dve.wait_ge(s_vc, steps[0])
            dve.wait_ge(s_const, 2)
            for k in range(6):
                v.tensor_scalar(diag[:, k, :], identf[0:CG, 0:CG], dmm[:, k:k + 1], None, ALU.mult).then_inc(s_dmm, 1)
            link(v.tensor_tensor(step_d[:, :, :], dst_c[:, :, 1:CH + 1], dst_c[:, :, 0:CH], ALU.subtract))
            link(v.tensor_reduce(viol[:, 0:1], step_d[:, :, :], AX.XY, ALU.min))
            v.tensor_scalar(viol[:, 1:2], viol[:, 0:1], 0.0, None, ALU.is_lt).then_inc(s_viol, 1)
            dve.wait_ge(s_edge[4], 16)
            link(v.tensor_copy(ends_f[:, :, :], ends_i[:, :, :]))
            link(v.memset(base_f[:, 0:1], 0.0))
            link(v.memset(base_f[:, NG:NG + 1], float(NODES)))
            link(v.tensor_scalar(base_f[:, 1:NG], ends_f[:, 0, 0:NG - 1], 1.0, None, ALU.add))
            link(v.memset(ones1[:, :], 1.0))
            v.tensor_copy(base_i[0:1, 0:NG], base_f[:, 0:NG]).then_inc(s_base, 1)
            link(v.tensor_tensor(ends_f[:, 1, 0:NG - 1], ends_f[:, 0, 0:NG - 1], ends_f[:, 1, 0:NG - 1], ALU.is_ge))
            link(v.tensor_tensor(ends_f[:, 0, :], base_f[:, 1:NG + 1], base_f[:, 0:NG], ALU.subtract))
            link(v.tensor_reduce(vrow[:, 0:1], ends_f[:, 0, :], AX.X, ALU.max))
            link(v.tensor_reduce(vrow[:, 1:2], ends_f[:, 1, 0:NG - 1], AX.X, ALU.max))
            link(v.scalar_tensor_tensor(vrow[:, 2:3], vrow[:, 0:1], float(DW), vrow[:, 1:2], ALU.is_gt, ALU.add))
            dve.wait_ge(s_edge[2], 16)
            dve.wait_ge(s_edge[0], 16)
            dlow, srcf, shi = scr0, scr1, slo_f
            v.tensor_single_scalar(dlow[:, :].bitcast(i32), e_dst[:, :], DW - 1, op=ALU.bitwise_and).then_inc(s_vc, 1)
            steps[0] += 1
            link(v.tensor_copy(srcf[:, :], e_src[:, :]))
            link(v.tensor_scalar(shi[:, :], srcf[:, :], float(SLO), None, ALU.is_ge))
            link(v.scalar_tensor_tensor(key_f[:, :], e_dst[:, :], 2.0, dlow[:, :].bitcast(i32), ALU.mult, ALU.subtract))
            link(v.scalar_tensor_tensor(key_f[:, :], shi[:, :], float(DW), key_f[:, :], ALU.mult, ALU.add))
            link(v.scalar_tensor_tensor(slo_f[:, :], shi[:, :], -float(SLO), srcf[:, :], ALU.mult, ALU.add))
            dve.wait_ge(s_bc, 2)
            dve.wait_ge(s_const, 6)
            link(v.tensor_scalar(hit[:, :], psX[1][0:NWIN, 0:NCH], wlim[:, 0:1], None, ALU.is_ge))
            link(v.scalar_tensor_tensor(hit[:, :], psX[0][0:NWIN, 0:NCH], wlim[:, 1:2], hit[:, :], ALU.is_le, ALU.mult))
            v.tensor_tensor(hit2[:, :], hit[:, :], c_dn[:, :], ALU.mult).then_inc(s_vc, 1)
            steps[0] += 1
            link(v.tensor_tensor(hit[:, :], hit[:, :], c_up[:, :], ALU.mult))
            v.tensor_reduce(rcol[:, 0:1], hit2[:, :], AX.X, ALU.max).then_inc(s_vc, 1)
            steps[0] += 1
            link(v.tensor_reduce(rcol[:, 1:2], hit[:, :], AX.X, ALU.max))
            link(v.tensor_scalar(rcol[:, 2:3], rcol[:, 0:1], -1.0, float(NCH), ALU.mult, ALU.add))
            link(v.tensor_scalar(rcol[:, 2:3], rcol[:, 2:3], float(NCH - 3), None, ALU.min))
            link(v.tensor_tensor(rcol[:, 3:4], rcol[:, 1:2], rcol[:, 2:3], ALU.subtract))
            v.tensor_scalar(rcol[:, 3:4], rcol[:, 3:4], 3.0, None, ALU.max).then_inc(s_rcol, 1)
            dve.wait_ge(s_edge[3], 16)
            link(v.memset(wq[:, :, NQ - 1], 1.0))
            link(v.tensor_copy(wq[:, :, 0], e_w[:, :]))
            link(v.tensor_tensor(scr0[:, :], e_w[:, :], wq[:, :, 0], ALU.subtract))
            link(v.tensor_copy(wq[:, :, 1], scr0[:, :]))
            link(v.tensor_tensor(scr0[:, :], scr0[:, :], wq[:, :, 1], ALU.subtract))
            link(v.tensor_copy(wq[:, :, 2], scr0[:, :]))
            dve.wait_ge(s_bb, 1)
            bb = psX[1][:, 0:NG]
            for part in range(2):
                if part == 0:
                    def cut(a):
                        return a[:, 0:NCH].rearrange("p (g k) -> p g k", k=GC)
                    kk, n = key_g[:, :, 0:GC], GC
                else:
                    def cut(a):
                        return a[:, GC:NCP].rearrange("p (g k) -> p g k", k=GC)[:, :, 0:1]
                    kk, n = key_g[:, :, GC:GC + 1], 1
                rel = scr0[:, 0:NG * n].rearrange("p (g k) -> p g k", k=n)
                fit = scr1[:, 0:NG * n].rearrange("p (g k) -> p g k", k=n)
                link(v.tensor_tensor(rel, cut(e_dst), bb.unsqueeze(2).to_broadcast([CH, NG, n]), ALU.subtract))
                link(v.tensor_scalar(fit, rel, 0.0, None, ALU.is_ge))
                link(v.scalar_tensor_tensor(fit, rel, float(DW), fit, ALU.is_lt, ALU.mult))
                link(v.tensor_scalar(kk, cut(e_src), float(SLO), float(DW), ALU.is_ge, ALU.mult))
                link(v.tensor_tensor(kk, kk, rel, ALU.add))
                link(v.scalar_tensor_tensor(kk, kk, 1.0, fit, ALU.add, ALU.mult))
            link(v.tensor_tensor(vrow[:, 3:4], psX[1][0:1, 500:501], vrow[:, 2:3], ALU.add))
            link(v.tensor_scalar(flag_i[:, :], vrow[:, 3:4], 0.5, None, ALU.is_lt))
            dve.wait_ge(s_rrow, 1)
            v.tensor_copy(rng[0:1, :].rearrange("p (w k) -> p k w", k=4)[:, 0:3, :],
                          psX[0][0:1, 0:3 * NWIN].rearrange("p (k w) -> p k w", k=3)).then_inc(s_rng, 1)
            dve.wait_ge(s_rng, 1)
            for p in range(P_IN):
                wh = W[p // 2][:, 2 * (p % 2):2 * (p % 2) + 2, :, :]
                split_lo(p % 2, p, (wh[:, :, 0, :], wh[:, :, 1, :]))
            dve.wait_ge(s_small, 80)
            link(v.tensor_scalar(gate[:, :, 0, :], gate_raw[:, :, :], WS, None, ALU.mult))
            link(v.scalar_tensor_tensor(gate[:, :, 1, :], gate_raw[:, :, :], WS, gate[:, :, 0, :], ALU.mult,
                                        ALU.subtract))
            link(v.memset(ones16[:, :], 1.0))
            dve.wait_ge(s_const, 10)
            v.memset(marks[:, 6:7], 0.0).then_inc(oh_free, NB)
            v.memset(marks[:, 0:1], 0.0).then_inc(g_lo, AHEAD)
            v.memset(marks[:, 1:2], 0.0).then_inc(g_q, NKR)
            v.memset(marks[:, 2:3], 0.0).then_inc(g_sum, NKR)
            v.memset(marks[:, 3:4], 0.0).then_inc(g_rc, AHEAD)
            v.memset(marks[:, 4:5], 0.0).then_inc(g_hi, 1)
            v.memset(marks[:, 5:6], 0.0).then_inc(g_start, 1)
            v.memset(marks[:, 7:8], 0.0).then_inc(s_flag, 1)
            fast = dve.value_load(flag_i[0:1, 0:1])

            def source(slot, c):
                v.tensor_scalar(oh_src[:, slot * SLP:(slot + 1) * SLP], iota_s[:, :], slo_f[:, ds(c, 1)], None,
                                ALU.is_equal).then_inc(g_oh, 1)

            def group(u, n):
                dve.wait_ge(g_sum, n + 2)
                for k in range(1, GC + 1):
                    source((u * GC + k) % NOH, n * GC + k)
                dve.wait_ge(g_q, n + 1)
                v.tensor_tensor(eq[:, u % NKR], iota_k[:, 1:KEYS + 1].unsqueeze(1).to_broadcast([CH, 4, KEYS]),
                                key_g[:, ds(n, 1), :].rearrange("p o c -> p (o c)").unsqueeze(2).to_broadcast(
                                    [CH, 4, KEYS]), ALU.is_equal).then_inc(g_eq, 1)

            def low(i, n, b):
                dve.wait_ge(g_hi, n + 2)
                dve.wait_ge(g_lo, n + AHEAD)
                v.tensor_tensor(AT_l[:, :, 0, ds(b, DW)],
                                psT[i][0:PT, 0:320].rearrange("p (j m d) -> p m j d", m=2, d=DW)[:, 0],
                                AT_h[:, :, 0, ds(b, DW)], ALU.subtract).then_inc(g_lo, 1)

            def base(eng, n):
                return eng.value_load(base_i[0:1, ds(n, 1)]).with_bounds(min_val=0, max_val=NODES)

            with dve.If(fast > 0):
                dve.wait_ge(g_start, 1)
                source(0, 0)
                for n in range(3):
                    group(n, n)
                with dve.Fori(0, (NG - 6) // 6) as i:
                    for u in range(6):
                        group(u + 3, i * 6 + (u + 3))
                        low(u % 2, i * 6 + u, base(dve, i * 6 + u))
                for n in range(NG - 3, NG):
                    group(n, n)
                    low((n - 3) % 2, n - 3, base(dve, n - 3))
                for n in range(NG - 3, NG):
                    low(n % 2, n, base(dve, n))
            with dve.Else():
                with dve.Fori(0, NWIN) as w:
                    c0 = dve.value_load(rng[0:1, ds(4 * w, 1)], min_val=0, max_val=NCH - 3)
                    cnt = dve.value_load(rng[0:1, ds(4 * w + 1, 1)], min_val=3, max_val=NCH)
                    n0 = dve.value_load(rng[0:1, ds(4 * w + 2, 1)], min_val=0, max_val=NCH * NWIN)
                    with dve.Fori(0, cnt) as k:
                        c = dve.snap(c0 + k).with_bounds(min_val=0, max_val=NCH - 1)
                        slot = dve.snap((n0 + k) % NB, min_val=0, max_val=NB - 1)
                        dve.wait_ge(oh_free, n0 + k + 1)
                        v.tensor_scalar(oh_src[:, ds(slot * SLP, SLP)], iota_s[:, :], slo_f[:, ds(c, 1)], None,
                                        ALU.is_equal)
                        v.scalar_tensor_tensor(
                            oh_key[:, ds(slot * 128, 128)].rearrange("p (q k) -> p q k", q=NQ),
                            iota_k[:, ds(w * KEYS, KEYS)].unsqueeze(1).to_broadcast([CH, NQ, KEYS]),
                            key_f[:, ds(c, 1)],
                            wq[:, ds(c, 1), :].rearrange("p o q -> p (o q)").unsqueeze(2).to_broadcast([CH, NQ, KEYS]),
                            ALU.is_equal, ALU.mult).then_inc(oh_ready, 1)

            dve.wait_ge(s_x, 16)
            row_stats(x_sb)
            link(v.tensor_copy(rs[:, :], rx[:, 0:NT]))
            dve.wait_ge(s_deg, 1)
            link(v.tensor_scalar(rx[:, :], psX[0][0:PT, 0:2 * NT], 1.0, None, ALU.add))
            link(v.tensor_scalar(pos[:, :], rx[:, :], 0.0, None, ALU.is_gt))
            link(v.tensor_tensor(rx[:, :], rx[:, :], pos[:, :], ALU.mult))
            link(v.tensor_scalar(rw[:, :], pos[:, :], -1.0, 1.0, ALU.mult, ALU.add))
            rsqrt(v.tensor_tensor(rv[:, :], rx[:, :], rw[:, :], ALU.add), 2 * NT)
            link(v.tensor_tensor(dis[:, :], rx[:, :], pos[:, :], ALU.mult))
            link(v.tensor_scalar(dsc[:, :], dis[:, :], 1.0 / WS, None, ALU.mult))
            link(v.tensor_tensor(rs[:, :], rs[:, :], dis[:, 0:NT], ALU.mult))

            def rows_lo(i, t, n):
                dve.wait_ge(xs_hi, n + 1)
                v.tensor_tensor(xs[:, ds(t, 1), 1, :].rearrange("p o n -> p (o n)"), xt[i][:, :],
                                xs[:, ds(t, 1), 0, :].rearrange("p o n -> p (o n)"), ALU.subtract).then_inc(xs_lo, 1)

            for t in range(NT):
                if t >= 2:
                    rows_lo(t % 2, t - 2, t - 2)
                    dve.wait_ge(xs_lo, t - 1)
                v.tensor_scalar(xt[t % 2][:, :], x_sb[:, t, :], mv[:, t, 0:1], rs[:, t:t + 1], ALU.subtract,
                                ALU.mult).then_inc(xt_ready, 1)
            rows_lo(0, NT - 2, NT - 2)
            rows_lo(1, NT - 1, NT - 1)

            def agg_low(layer):
                for c in range(CT):
                    ps = agg_ps[c % 2]
                    n = layer * CT + c
                    dve.wait_ge(agg_hi, n + 1)
                    v.tensor_tensor(aggT[:, c, 1, 0:1000].rearrange("p (a n) -> p a n", a=2),
                                    ps[0][:, :].rearrange("p (a n) -> p a n", a=2)[:, :, 0:500],
                                    aggT[:, c, 0, 0:1000].rearrange("p (a n) -> p a n", a=2), ALU.subtract)
                    v.tensor_tensor(aggT[:, c, 1, 1000:NODES], ps[1][:, 0:250], aggT[:, c, 0, 1000:NODES],
                                    ALU.subtract).then_inc(agg_lo, 1)

            agg_low(0)
            for t in range(NT):
                if t >= 2:
                    rows_lo(t % 2, t - 2, NT + t - 2)
                    dve.wait_ge(xs_lo, NT + t - 1)
                dve.wait_ge(lin_full, t + 1)
                v.scalar_tensor_tensor(xt[t % 2][:, :], psX[t % 2][0:PT, :], dsc[:, t:t + 1], b_bc[0][:, :], ALU.mult,
                                       ALU.add).then_inc(lin_read, 1)
                dve.wait_ge(lin_read, t + 1)
                v.tensor_scalar(xt[t % 2][:, :], xt[t % 2][:, :], 0.0, dis[:, NT + t:NT + t + 1], ALU.max,
                                ALU.mult).then_inc(xt_ready, 1)
            rows_lo(0, NT - 2, 2 * NT - 2)
            rows_lo(1, NT - 1, 2 * NT - 1)
            agg_low(1)
            def in_piece(p):
                k, q = divmod(p - P_IN, 8)
                c, half = divmod(q, 2)
                wh = inW[1 - k][:, c:c + 1, :, half * 1024:half * 1024 + 1024]
                return wh[:, :, 0, :], wh[:, :, 1, :]

            for t in range(NT):
                dve.wait_ge(lin_full, NT + t + 1)
                v.scalar_tensor_tensor(xt[t % 2][:, :], psX[t % 2][0:PT, :], dsc[:, NT + t:NT + t + 1], b_bc[1][:, :],
                                       ALU.mult, ALU.add).then_inc(lin_read, 1)
                dve.wait_ge(lin_read, NT + t + 1)
                v.tensor_tensor(x_sb[:, t, :], x_sb[:, t, :], xt[t % 2][:, :], ALU.add).then_inc(s_vc, 1)
                steps[0] += 1
                if t > 1:
                    split_lo(t % 2, P_IN + t - 2, in_piece(P_IN + t - 2))
            dve.wait_ge(s_vc, steps[0])

            row_stats(x_sb)
            for t in range(NT):
                last = v.tensor_scalar(zf[:, t, :], x_sb[:, t, :], mv[:, t, 0:1], rx[:, t:t + 1], ALU.subtract, ALU.mult)
            link(last)
            row_stats(zf)
            for t in range(NT):
                v.tensor_scalar(zf[:, t, :], zf[:, t, :], mv[:, t, 0:1], rx[:, t:t + 1], ALU.subtract,
                                ALU.mult).then_inc(zf_ready, 1)

            def flat_lo(t):
                dve.wait_ge(fl_hi, t + 1)
                v.tensor_tensor(flatT[:, :, 1, t * PT:(t + 1) * PT], vt[t % 2][:, :].rearrange("p (c n) -> p c n", c=CT),
                                flatT[:, :, 0, t * PT:(t + 1) * PT], ALU.subtract).then_inc(fl_lo, 1)

            for t in range(NT):
                if t >= 2:
                    flat_lo(t - 2)
                    dve.wait_ge(fl_lo, t - 1)
                dve.wait_ge(tr_full, t + 1)
                vv = vt[t % 2][:, :].rearrange("p (c n) -> p c n", c=CT)
                link(v.tensor_tensor(vv, psX[t % 2][:, 0:CT * PT].rearrange("p (c n) -> p c n", c=CT),
                                     lnw[:, 0, :].unsqueeze(2).to_broadcast([128, CT, PT]), ALU.mult))
                v.tensor_tensor(vv, vv, lnw[:, 1, :].unsqueeze(2).to_broadcast([128, CT, PT]), ALU.add).then_inc(
                    vt_ready, 1)
            flat_lo(NT - 2)
            flat_lo(NT - 1)
            for p in range(P_IN + 8, P_OUT):
                split_lo(p % 2, p, in_piece(p))

            gb = gb10[:, :].unsqueeze(1).to_broadcast([PT, NT, 10])
            es, pr, cand, oh = e4
            gs, mx, den, p2, t1 = r1

            def wide(a):
                return a[:, :].unsqueeze(2).to_broadcast([PT, NT, 4])

            i4b = i4[:, :].unsqueeze(1).to_broadcast([PT, NT, 4])
            dve.wait_ge(s_logit, 1)
            link(v.scalar_tensor_tensor(lg[:, :, :], psT[0][0:PT, 0:NT * 10].rearrange("p (t k) -> p t k", k=10),
                                        1.0 / WS, gb, ALU.mult, ALU.add))
            link(v.tensor_tensor(gs[:, :], lg[:, :, 1], lg[:, :, 0], ALU.is_gt))
            link(v.tensor_scalar(t1[:, :], gs[:, :], -1.0, 1.0, ALU.mult, ALU.add))
            link(v.tensor_tensor(es[:, :, :], lg[:, :, 2:6], wide(t1), ALU.mult))
            link(v.tensor_tensor(pr[:, :, :], lg[:, :, 6:10], wide(gs), ALU.mult))
            link(v.tensor_tensor(es[:, :, :], es[:, :, :], pr[:, :, :], ALU.add))
            link(v.tensor_reduce(mx[:, :], es[:, :, :], AX.X, ALU.max))
            v.tensor_tensor(es[:, :, :], es[:, :, :], wide(mx), ALU.subtract).then_inc(s_exin, 1)
            dve.wait_ge(s_exout, 1)
            link(v.tensor_reduce(den[:, :], es[:, :, :], AX.X, ALU.add))
            link(v.reciprocal(den[:, :], den[:, :]))
            link(v.tensor_tensor(pr[:, :, :], es[:, :, :], wide(den), ALU.mult))

            def top(best, onehot):
                link(v.tensor_reduce(best[:, :], pr[:, :, :], AX.X, ALU.max))
                link(v.tensor_tensor(cand[:, :, :], pr[:, :, :], wide(best), ALU.is_equal))
                link(v.tensor_tensor(cand[:, :, :], cand[:, :, :], i4b, ALU.mult))
                link(v.tensor_reduce(den[:, :], cand[:, :, :], AX.X, ALU.max))
                link(v.tensor_tensor(onehot, cand[:, :, :], wide(den), ALU.is_equal))

            top(mx, oh[:, :, :])
            link(v.scalar_tensor_tensor(pr[:, :, :], oh[:, :, :], -2.0, pr[:, :, :], ALU.mult, ALU.add))
            top(p2, es[:, :, :])
            link(v.scalar_tensor_tensor(den[:, :], mx[:, :], 1e-8, p2[:, :], ALU.add, ALU.add))
            link(v.reciprocal(den[:, :], den[:, :]))
            link(v.tensor_tensor(mx[:, :], mx[:, :], den[:, :], ALU.mult))
            link(v.tensor_tensor(p2[:, :], p2[:, :], den[:, :], ALU.mult))
            link(v.tensor_tensor(pr[:, :, :], oh[:, :, :], wide(mx), ALU.mult))
            link(v.tensor_tensor(cand[:, :, :], es[:, :, :], wide(p2), ALU.mult))
            link(v.tensor_tensor(pr[:, :, :], pr[:, :, :], cand[:, :, :], ALU.add))
            link(v.tensor_tensor(oh[:, :, :], oh[:, :, :], es[:, :, :], ALU.add))
            link(v.tensor_scalar(pr[:, :, :], pr[:, :, :], 1.0 / (WS * HS), None, ALU.mult))
            link(v.memset(cnt9[:, :, NE], 1.0))
            link(v.tensor_tensor(comb8[:, :, 0:4], pr[:, :, :], wide(t1), ALU.mult))
            link(v.tensor_tensor(comb8[:, :, 4:8], pr[:, :, :], wide(gs), ALU.mult))
            link(v.tensor_tensor(cnt9[:, :, 0:4], oh[:, :, :], wide(t1), ALU.mult))
            v.tensor_tensor(cnt9[:, :, 4:8], oh[:, :, :], wide(gs), ALU.mult).then_inc(s_route, 1)

            def hidden(k, g, n, jt):
                i = g % 2
                a0, width = SPANS[g % 3]
                dve.wait_ge(in_silu, n + 1)
                v.scalar_tensor_tensor(sl[i][:, 0:width], in_ps[i][:, 512:512 + width], HS / WS, sl[i][:, 0:width],
                                       ALU.mult, ALU.mult).then_inc(in_h, 1)
                dve.wait_ge(h_hi, n + 1)
                v.tensor_tensor(hT[k][:, ds(jt, 1), 1, a0:a0 + width].rearrange("p o n -> p (o n)"), sl[i][:, 0:width],
                                hT[k][:, ds(jt, 1), 0, a0:a0 + width].rearrange("p o n -> p (o n)"),
                                ALU.subtract).then_inc(h_lo, 1)

            v.memset(scr_mark[:, 0:1], 0.0).then_inc(in_h, AHEAD)
            v.memset(scr_mark[:, 1:2], 0.0).then_inc(h_lo, AHEAD)
            for k in (1, 0):
                with dve.Fori(0, 4) as jp:
                    for g in range(6):
                        hidden(k, g, jp * 6 + ((1 - k) * 24 + g), jp * 2 + g // 3)

            dve.wait_ge(s_cntT, 1)
            for b in range(3):
                last = v.tensor_copy(cntT[:, b * 4 * PT:min(NT, b * 4 + 4) * PT],
                                     (psT[0], psT[1], psX[0])[b][0:9, 0:min(4, NT - 4 * b) * PT])
            last.then_inc(s_cntTc, 1)

            def out_piece(slot, q):
                wh = outW[slot][:, 2 * q:2 * q + 2, :, :]
                return wh[:, :, 0, :], wh[:, :, 1, :]

            for q in range(4):
                split_lo(q % 2, P_OUT + q, out_piece(0, q))
            for e in range(2):
                for q in range(4):
                    split_lo(q % 2, P_EXP + 4 * e + q, out_piece(1 + e, q))
            for t in range(NT):
                dve.wait_ge(out_full, 2 * t + 1)
                v.scalar_tensor_tensor(x_sb[:, t, :], psX[0][0:PT, :], 1.0 / (WS * HS), x_sb[:, t, :], ALU.mult,
                                       ALU.add).then_inc(out_read, 1)
                dve.wait_ge(out_full, 2 * t + 2)
                dve.wait_ge(out_read, 2 * t + 1)
                v.tensor_tensor(x_sb[:, t, :], x_sb[:, t, :], psX[1][0:PT, :], ALU.add).then_inc(out_read, 1)
            def expert_tile(i, e, t, n):
                dve.wait_ge(out_full, 2 * NT + n + 1)
                dve.wait_ge(out_read, 2 * NT + n)
                xv = x_sb[:, ds(t, 1), :].rearrange("p o n -> p (o n)")
                return v.scalar_tensor_tensor(xv, psX[i][0:PT, :], comb8[:, ds(t, 1), ds(e, 1)].rearrange("p o n -> p (o n)"),
                                              xv, ALU.mult, ALU.add)
            def expert_pair(ep, more):
                for u in range(2):
                    with dve.Fori(0, NT // 2) as tp:
                        for i in range(2):
                            n = ep * (2 * NT) + tp * 2 + (u * NT + i)
                            expert_tile(i, ep * 2 + u, tp * 2 + i, n).then_inc(out_read, 1)
                    if more:
                        for q in range(4):
                            split_lo(q % 2, ep * 8 + (P_EXP + 8 + 4 * u + q), out_piece(1 + u, q))

            with dve.Fori(0, NE // 2 - 1) as ep:
                expert_pair(ep, True)
            expert_pair(NE // 2 - 1, False)
            dve.wait_ge(out_read, 2 * NT + NE * NT)
            v.memset(scr_mark[:, 2:3], 0.0).then_inc(s_final, NT)

        @block.tensor
        def _(pe):
            t = nc.tensor
            pe.wait_ge(s_dmm, 6)
            pe.wait_ge(s_const, 2)
            for k in range(6):
                last = t.matmul(psX[k // 3][0:NWIN, (k % 3) * CG:(k % 3 + 1) * CG], onesf[0:CG, 0:NWIN],
                                diag[:, k, :], start=True, stop=True)
                if k % 3 == 2:
                    last.then_inc(s_bc, 1)
            pe.wait_ge(s_viol, 1)
            pe.wait_ge(s_rcol, 1)
            pe.wait_ge(s_base, 1)
            t.matmul(psX[1][0:1, 500:501], viol[:, 1:2], onesf[0:CG, 0:1], start=True, stop=True)
            t.matmul(psX[1][:, 0:NG], ones1[:, :], base_f[:, 0:NG], start=True, stop=True).then_inc(s_bb, 1)
            pe.wait_ge(s_const, 3)
            t.matmul(psX[0][0:1, 0:NWIN], rcol[:, 2:3], identf[0:NWIN, 0:NWIN], start=True, stop=True)
            t.matmul(psX[0][0:1, NWIN:2 * NWIN], rcol[:, 3:4], identf[0:NWIN, 0:NWIN], start=True, stop=True)
            t.matmul(psX[0][0:1, 2 * NWIN:3 * NWIN], rcol[:, 3:4], tri[0:NWIN, 0:NWIN], start=True,
                     stop=True).then_inc(s_rrow, 1)
            pe.wait_ge(s_rng, 1)
            pe.wait_ge(s_const, 10)

            def window(i, w):
                pe.wait_ge(r_copied, w + 1)
                cnt = pe.value_load(rng[0:1, ds(4 * w + 1, 1)], min_val=3, max_val=NCH)
                n0 = pe.value_load(rng[0:1, ds(4 * w + 2, 1)], min_val=0, max_val=NCH * NWIN)

                def step(k, start, stop):
                    slot = pe.snap((n0 + k) % NB, min_val=0, max_val=NB - 1)
                    pe.wait_ge(oh_ready, n0 + k + 1)
                    for h in range(2):
                        last = t.matmul(psR[i][:, h * 512:h * 512 + HW2], oh_key[:, ds(slot * 128, 128)],
                                        oh_src[:, ds(slot * SLP + h * HW2, HW2)], start=start, stop=stop)
                    last.then_inc(oh_free, 1)
                    return last
                step(0, True, False)
                with pe.Fori(1, cnt - 1) as k:
                    step(k, False, False)
                step(cnt - 1, False, True)
                t.matmul(psX[1][:, 0:1], ident[:, :], ident[:, 0:1], start=True, stop=True).then_inc(r_full, 1)

            def combine(i, w):
                pe.wait_ge(r_copied, AHEAD + w + 1)
                pe.wait_ge(t_copied, w + 1)
                for j in range(5):
                    last = t.matmul(psT[i][0:PT, j * 64:j * 64 + 64], R[i][:, j * PT:(j + 1) * PT], comb[:, :],
                                    start=True, stop=True)
                last.then_inc(t_full, 1)

            pe.wait_ge(s_flag, 1)
            fast = pe.value_load(flag_i[0:1, 0:1])

            def sums(u, n):
                pe.wait_ge(g_oh, n * GC + (GC + 1))
                pe.wait_ge(g_q, n + (NKR + 1))
                pe.wait_ge(g_rc, n + 1)
                for k in range(GC + 1):
                    c = (u * GC + k) % NOH
                    for h in range(2):
                        last = t.matmul(psR[u % 2][:, h * 512:h * 512 + HW2],
                                        oh_key[:, (u % NKR) * 512 + k * 128:(u % NKR) * 512 + (k + 1) * 128],
                                        oh_src[:, c * SLP + h * HW2:c * SLP + (h + 1) * HW2], start=(k == 0),
                                        stop=(k == GC))
                last.then_inc(g_sum, 1)

            def parts(i, n):
                pe.wait_ge(g_rc, n + (AHEAD + 1))
                pe.wait_ge(g_lo, n + 1)
                for j in range(5):
                    last = t.matmul(psT[i][0:PT, j * 64:j * 64 + 64], R[i][:, j * PT:(j + 1) * PT], comb[:, :],
                                    start=True, stop=True)
                last.then_inc(g_comb, 1)

            with pe.If(fast > 0):
                sums(0, 0)
                with pe.Fori(0, (NG - 6) // 6) as i:
                    for u in range(6):
                        sums(u + 1, i * 6 + (u + 1))
                        parts(u % 2, i * 6 + u)
                for n in range(NG - 6, NG - 1):
                    sums(n + 1, n + 1)
                    parts(n % 2, n)
                parts(1, NG - 1)
                pe.wait_ge(g_lo, AHEAD + NG)
                pe.wait_ge(g_zero, 1)
            with pe.Else():
                t.matmul(psX[1][:, 0:1], ident[:, :], ident[:, 0:1], start=True, stop=True).then_inc(t_full, AHEAD)
                window(0, 0)
                with pe.Fori(0, (NWIN - 1) // 2) as i:
                    window(1, 2 * i + 1)
                    combine(0, 2 * i)
                    window(0, 2 * i + 2)
                    combine(1, 2 * i + 1)
                combine(0, NWIN - 1)
                pe.wait_ge(at_ready, AHEAD + NWIN)

            with pe.Fori(0, NT) as j:
                for m in range(2):
                    for k in range(2 * NT):
                        A = (AT_h, AT_l)[k % 2]
                        last = t.matmul(psX[0][0:PT, ds(j + m * NT, 1)], A[:, k // 2, m, ds(j * PT, PT)],
                                        ones16[:, :], start=(k == 0), stop=(k == 2 * NT - 1))
            t.matmul(psX[1][:, 0:1], ident[:, :], ident[:, 0:1], start=True, stop=True).then_inc(s_deg, 1)

            def aggregate(layer):
                pe.wait_ge(xs_lo, (layer + 1) * NT)
                for c in range(CT):
                    n = layer * CT + c
                    if n >= 2:
                        pe.wait_ge(agg_lo, n - 1)
                    ps = agg_ps[c % 2]
                    outs = (ps[0][:, 0:500], ps[0][:, 512:1012], ps[1][:, 0:250])
                    for jj in range(NT):
                        j = (jj % 2) * 5 + jj // 2
                        for hl in range(2):
                            lhs = xs[:, j, hl, c * 128:(c + 1) * 128]
                            for A in ((AT_h, AT_l) if hl == 0 else (AT_h,)):
                                for b, (a0, width) in enumerate(SPANS):
                                    last = t.matmul(outs[b], lhs, A[:, jj, layer, a0:a0 + width],
                                                    start=(jj == 0 and hl == 0 and A is AT_h),
                                                    stop=(jj == NT - 1 and hl == 1))
                    for j in range(NT):
                        for hl in range(2):
                            last = t.matmul(outs[j // 4][:, (j % 4) * PT:(j % 4 + 1) * PT],
                                            xs[:, j, hl, c * 128:(c + 1) * 128], ident[0:PT, 0:PT], start=False,
                                            stop=False, skip_group_check=True)
                    last.then_inc(agg_full, 1)

            def linear(layer):
                pe.wait_ge(w_lo, P_IN)
                pe.wait_ge(agg_lo, (layer + 1) * CT)
                for tile in range(NT):
                    n = layer * NT + tile
                    if n >= 2:
                        pe.wait_ge(lin_read, n - 1)
                    k = 0
                    for c in range(CT):
                        for hl, wl in ((0, 0), (0, 1), (1, 0)):
                            last = t.matmul(psX[tile % 2][0:PT, :], aggT[:, c, hl, tile * PT:(tile + 1) * PT],
                                            W[layer][:, c, wl, :], start=(k == 0), stop=(k == 3 * CT - 1))
                            k += 1
                    last.then_inc(lin_full, 1)

            aggregate(0)
            linear(0)
            aggregate(1)
            linear(1)

            pe.wait_ge(lin_read, 2 * NT)
            for tile in range(NT):
                pe.wait_ge(zf_ready, tile + 1)
                if tile >= 2:
                    pe.wait_ge(vt_ready, tile - 1)
                for c in range(CT):
                    last = t.transpose(psX[tile % 2][:, c * PT:(c + 1) * PT], zf[:, tile, c * 128:(c + 1) * 128],
                                       identf[0:PT, 0:PT])
                last.then_inc(tr_full, 1)
            pe.wait_ge(fl_lo, NT)
            for tile in range(NT):
                k = 0
                for c in range(CT):
                    for hl, wl in ((0, 0), (0, 1), (1, 0)):
                        last = t.matmul(psT[0][0:PT, tile * 10:tile * 10 + 10],
                                        flatT[:, c, hl, tile * PT:(tile + 1) * PT], gate[:, c, wl, :],
                                        start=(k == 0), stop=(k == 3 * CT - 1))
                        k += 1
            last.then_inc(s_logit, 1)

            def hidden(k, g, n, jt):
                i = g % 2
                a0, width = SPANS[g % 3]
                pe.wait_ge(in_h, n + 1)
                for half in range(2):
                    m = 0
                    for c in range(CT):
                        for hl, wl in ((0, 0), (1, 0), (0, 1)):
                            last = t.matmul(in_ps[i][:, half * 512:half * 512 + width],
                                            inW[k][:, c, wl, ds(jt * 128 + half * HID, 128)],
                                            flatT[:, c, hl, a0:a0 + width], start=(m == 0), stop=(m == 3 * CT - 1))
                            m += 1
                last.then_inc(in_full, 1)

            for k in (1, 0):
                pe.wait_ge(w_lo, P_IN + 8 * (2 - k))
                with pe.Fori(0, 4) as jp:
                    for g in range(6):
                        n = jp * 6 + ((1 - k) * 24 + g)
                        hidden(k, g, n, jp * 2 + g // 3)
            pe.wait_ge(s_route, 1)
            pe.wait_ge(h_lo, AHEAD + 48)
            for tile in range(NT):
                last = t.transpose((psT[0], psT[1], psX[0])[tile // 4][0:9, (tile % 4) * PT:(tile % 4 + 1) * PT],
                                   cnt9[:, tile, :], identf[0:PT, 0:PT])
            last.then_inc(s_cntT, 1)
            pe.wait_ge(s_cntTc, 1)

            def project(k, ps, tile, slot):
                m = 0
                for j in range(8):
                    for hl, wl in ((0, 0), (0, 1), (1, 0)):
                        last = t.matmul(ps[0:PT, :], hT[k][:, j, hl, ds(tile * PT, PT)], outW[slot][:, j, wl, :],
                                        start=(m == 0), stop=(m == 23))
                        m += 1
                return last
            pe.wait_ge(w_lo, P_OUT + 4)
            pe.wait_ge(s_bias, 16)
            for tile in range(NT):
                if tile:
                    pe.wait_ge(out_read, 2 * tile - 1)
                project(0, psX[0], tile, 0).then_inc(out_full, 1)
                if tile:
                    pe.wait_ge(out_read, 2 * tile)
                t.matmul(psX[1][0:PT, :], cntT[:, tile * PT:(tile + 1) * PT], bias9[:, :], start=True,
                         stop=True).then_inc(out_full, 1)
            with pe.Fori(0, NE // 2) as ep:
                for u in range(2):
                    with pe.Fori(0, NT // 2) as tp:
                        for i in range(2):
                            pe.wait_ge(w_lo, ep * 8 + (P_EXP + 4 * u + 4))
                            n = ep * (2 * NT) + tp * 2 + (u * NT + i)
                            pe.wait_ge(out_read, n + (2 * NT - 1))
                            project(1, psX[i], tp * 2 + i, 1 + u).then_inc(out_full, 1)

        @block.scalar
        def _(act):
            a = nc.scalar

            def split_hi(i, p, dst):
                act.wait_ge(s_w[i], (p // 2 + 1) * 16)
                a.activation(dst, raw[i][:, :].rearrange("p (a n) -> p a n", a=dst.shape[1]), ACT.Copy,
                             scale=WS).then_inc(w_hi, 1)

            for p in range(P_IN):
                split_hi(p % 2, p, W[p // 2][:, 2 * (p % 2):2 * (p % 2) + 2, 0, :])

            def evac_r(i, w):
                act.wait_ge(r_full, w + 1)
                act.wait_ge(t_full, w + 1)
                a.activation(R[i][:, :].rearrange("p (h s) -> p h s", h=2),
                             psR[i][:, :].rearrange("p (h s) -> p h s", h=2)[:, :, 0:HW2],
                             ACT.Copy).then_inc(r_copied, 1)

            def evac_t(i, w):
                act.wait_ge(t_full, AHEAD + w + 1)
                act.wait_ge(at_ready, w + 1)
                a.activation(T[i][:, :], psT[i][0:PT, 0:320], ACT.Copy).then_inc(t_copied, 1)

            act.wait_ge(s_flag, 1)
            fast = act.value_load(flag_i[0:1, 0:1])

            def copy_sums(i, n):
                act.wait_ge(g_sum, n + (NKR + 1))
                a.activation(R[i][:, :].rearrange("p (h s) -> p h s", h=2),
                             psR[i][:, :].rearrange("p (h s) -> p h s", h=2)[:, :, 0:HW2],
                             ACT.Copy).then_inc(g_rc, 1)

            def high(i, n, b):
                act.wait_ge(g_comb, n + 1)
                act.wait_ge(g_lo, n + AHEAD)
                a.activation(AT_h[:, :, :, ds(b, DW)], psT[i][0:PT, 0:320].rearrange("p (j m d) -> p j m d", m=2, d=DW),
                             ACT.Copy).then_inc(g_hi, 1)

            def act_base(n):
                return act.value_load(base_i[0:1, ds(n, 1)]).with_bounds(min_val=0, max_val=NODES)

            with act.If(fast > 0):
                copy_sums(0, 0)
                with act.Fori(0, (NG - 6) // 6) as i:
                    for u in range(6):
                        copy_sums((u + 1) % 2, i * 6 + (u + 1))
                        high(u % 2, i * 6 + u, act_base(i * 6 + u))
                for n in range(NG - 6, NG - 1):
                    copy_sums((n + 1) % 2, n + 1)
                    high(n % 2, n, act_base(n))
                high(1, NG - 1, act_base(NG - 1))
            with act.Else():
                act.wait_ge(s_const, 10)
                a.activation(amark[:, 0:1], ident[0:1, 0:1], ACT.Copy).then_inc(t_copied, AHEAD)
                a.activation(amark[:, 1:2], ident[0:1, 0:1], ACT.Copy).then_inc(r_copied, AHEAD)
                evac_r(0, 0)
                with act.Fori(0, (NWIN - 1) // 2) as i:
                    evac_r(1, 2 * i + 1)
                    evac_t(0, 2 * i)
                    evac_r(0, 2 * i + 2)
                    evac_t(1, 2 * i + 1)
                evac_t(0, NWIN - 1)

            def sqrt(n, calls):
                act.wait_ge(s_sqin, calls)
                a.activation(rw[:, 0:n], rv[:, 0:n], ACT.Sqrt).then_inc(s_sqout, 1)

            def rows_hi(layer):
                for t in range(NT):
                    act.wait_ge(xt_ready, layer * NT + t + 1)
                    a.activation(xs[:, t, 0, :], xt[t % 2][:, :], ACT.Copy).then_inc(xs_hi, 1)

            def agg_high(layer):
                for c in range(CT):
                    ps = agg_ps[c % 2]
                    act.wait_ge(agg_full, layer * CT + c + 1)
                    a.activation(aggT[:, c, 0, 0:1000].rearrange("p (a n) -> p a n", a=2),
                                 ps[0][:, :].rearrange("p (a n) -> p a n", a=2)[:, :, 0:500], ACT.Copy)
                    a.activation(aggT[:, c, 0, 1000:NODES], ps[1][:, 0:250], ACT.Copy).then_inc(agg_hi, 1)

            sqrt(NT, 1)
            sqrt(2 * NT, 2)
            rows_hi(0)
            agg_high(0)
            rows_hi(1)
            agg_high(1)
            for p in range(P_IN, P_IN + 8):
                k, q = divmod(p - P_IN, 8)
                split_hi(p % 2, p, inW[1 - k][:, q // 2:q // 2 + 1, 0, (q % 2) * 1024:(q % 2) * 1024 + 1024])
            sqrt(NT, 3)
            sqrt(NT, 4)
            for t in range(NT):
                act.wait_ge(vt_ready, t + 1)
                a.activation(flatT[:, :, 0, t * PT:(t + 1) * PT], vt[t % 2][:, :].rearrange("p (c n) -> p c n", c=CT),
                             ACT.Copy).then_inc(fl_hi, 1)
            for p in range(P_IN + 8, P_OUT):
                k, q = divmod(p - P_IN, 8)
                split_hi(p % 2, p, inW[1 - k][:, q // 2:q // 2 + 1, 0, (q % 2) * 1024:(q % 2) * 1024 + 1024])
            act.wait_ge(s_exin, 1)
            a.activation(e4[0][:, :, :], e4[0][:, :, :], ACT.Exp).then_inc(s_exout, 1)

            def hidden(k, g, n, jt):
                i = g % 2
                a0, width = SPANS[g % 3]
                act.wait_ge(in_full, n + 1)
                act.wait_ge(h_lo, n + 1)
                a.activation(sl[i][:, 0:width], in_ps[i][:, 0:width], ACT.Silu, scale=1.0 / WS).then_inc(in_silu, 1)
                act.wait_ge(in_h, AHEAD + n + 1)
                a.activation(hT[k][:, ds(jt, 1), 0, a0:a0 + width].rearrange("p o n -> p (o n)"), sl[i][:, 0:width],
                             ACT.Copy).then_inc(h_hi, 1)

            for k in (1, 0):
                with act.Fori(0, 4) as jp:
                    for g in range(6):
                        hidden(k, g, jp * 6 + ((1 - k) * 24 + g), jp * 2 + g // 3)
            for q in range(4):
                split_hi(q % 2, P_OUT + q, outW[0][:, 2 * q:2 * q + 2, 0, :])
            for e in range(2):
                for q in range(4):
                    split_hi(q % 2, P_EXP + 4 * e + q, outW[1 + e][:, 2 * q:2 * q + 2, 0, :])
            with act.Fori(0, NE // 2 - 1) as ep:
                for u in range(2):
                    act.wait_ge(out_full, ep * (2 * NT) + (2 * NT + (u + 1) * NT))
                    for q in range(4):
                        act.wait_ge(s_w[q % 2], ep * 64 + ((P_EXP + 8 + 4 * u + q) // 2 + 1) * 16)
                        a.activation(outW[1 + u][:, 2 * q:2 * q + 2, 0, :], raw[q % 2][:, :].rearrange("p (a n) -> p a n", a=2),
                                     ACT.Copy, scale=WS).then_inc(w_hi, 1)


_OUT_ROWS = NODES
DEBUG = False


def kernel(**inputs):
    import numpy as np
    import concourse.bacc as _bacc
    from concourse import mybir as _mybir
    from concourse.bass_utils import run_bass_kernel_spmd as _run

    nc = _bacc.Bacc("TRN2", target_bir_lowering=False, num_devices=1)
    arrays, io = {}, {}

    def give(name, a):
        a = np.ascontiguousarray(a)
        arrays[f"in_{name}"] = a
        io[name] = nc.dram_tensor(f"in_{name}", a.shape, _mybir.dt.from_np(a.dtype), kind="ExternalInput").ap()

    def padded(a, fill):
        return np.concatenate([a, np.full(NCP * CH - EDGES, fill, a.dtype)])

    src, dst = padded(inputs["src"], 4000), padded(inputs["dst"], 2 * NODES)
    give("e_src", src.reshape(NCP, CH).T)
    give("e_dst", dst.reshape(NCP, CH).T)
    give("e_w", padded(inputs["edge_weight"], 0).reshape(NCP, CH).T)
    by_chunk = np.concatenate([dst.reshape(NCP, CH)[:NCH], dst.reshape(NCP, CH)[1:NCH + 1, :1]], axis=1)
    give("dst_c", by_chunk.reshape(3, CG, CH + 1).transpose(1, 0, 2))
    by_group = dst.reshape(NCP // GC, GC, CH)
    give("ends", np.stack([by_group[:NG, GC - 1, CH - 1], by_group[1:NG + 1, 0, CH - 1]])[None])
    give("x", inputs["x"].reshape(NT, PT, DIM).transpose(1, 0, 2))
    give("b1", inputs["L0_gnn_b1"])
    give("b2", inputs["L0_gnn_b2"])
    give("gb10", np.concatenate([inputs["L0_ffn_group_bias"], inputs["L0_ffn_expert_bias"]]))
    give("lnw", np.stack([inputs["L0_ffn_ln_scale"], inputs["L0_ffn_ln_bias"]]).reshape(2, CT, 128).transpose(2, 0, 1))
    gates = np.concatenate([inputs["L0_ffn_group_gate_w"], inputs["L0_ffn_expert_gate_w"]])
    give("gate", gates.T.reshape(CT, 128, 10).transpose(1, 0, 2))
    give("bias9", np.concatenate([inputs["L0_ffn_expert_out_bias"], inputs["L0_ffn_shared_out_b"][None]]))
    give("gw", np.stack([inputs[f"L0_gnn_W{i}"].reshape(2, 2, 128, DIM).transpose(0, 2, 1, 3).reshape(2, 128, 1024)
                         for i in (1, 2)]).reshape(4, 128, 1024))
    give("inw", np.stack([inputs[f"L0_ffn_{n}_in_w"].T.reshape(CT, 128, 2, 1024).transpose(0, 2, 1, 3)
                          for n in ("expert", "shared")]).reshape(16, 128, 1024))
    give("outw", inputs["L0_ffn_shared_out_w"].T.reshape(4, 2, 128, DIM).transpose(0, 2, 1, 3).reshape(4, 128, 1024))
    give("expw", inputs["L0_ffn_expert_out_weight"].transpose(0, 2, 1).reshape(NE, 4, 2, 128, DIM)
         .transpose(0, 1, 3, 2, 4).reshape(NE, 4, 128, 1024))
    out = nc.dram_tensor("out_0_dram", (_OUT_ROWS, DIM), _mybir.dt.float32, kind="ExternalOutput").ap()
    dbg = None
    if DEBUG:
        at = nc.dram_tensor("dbg_AT", (2, PT, NT, 2, DPAD), _mybir.dt.float16, kind="ExternalOutput").ap()
        rg = nc.dram_tensor("dbg_rng", (1, NWIN * 4), _mybir.dt.int32, kind="ExternalOutput").ap()
        dbg = {"AT": at, "rng": rg}
    gnn_ffn_kernel(nc, io, out, dbg)
    r = _run(nc, [arrays], core_ids=[0])
    return r.results[0]["out_0_dram"]
```
